# Optimizing a Trainium2 kernel written in Bass

```python
import numpy as np
import jax
import jax.numpy as jnp

def _softmax(x, axis=-1):
    return jax.nn.softmax(x, axis=axis)

def _gelu(x):
    return jax.nn.gelu(x, approximate=True)

def _silu(x):
    return jax.nn.silu(x)

def _sigmoid(x):
    return jax.nn.sigmoid(x)

def _layernorm(x, axis=-1, eps=1e-05):
    m = jnp.mean(x, axis=axis, keepdims=True)
    v = jnp.var(x, axis=axis, keepdims=True)
    return (x - m) / jnp.sqrt(v + eps)

def _scatter_add(tgt, idx, src, axis=0):
    return tgt.at[idx].add(src)

def _segment_sum(src, seg, n):
    return jax.ops.segment_sum(src, seg, n)
kernel_name = 'mk_macaron_d1_jaxref_r4_98a085'

def setup_inputs(seed: int=0):
    np.random.seed(seed)
    _w = jnp.asarray

    def _L0_attn_setup():
        import jax, jax.numpy as jnp
        import numpy as np
        B, T = (4, 512)
        D_MODEL = 256
        N_HEADS = 8
        HEAD_DIM = 64
        KV_LRANK = 64

        def _orthogonalize_per_head(w):
            chunks = w.reshape(N_HEADS, HEAD_DIM, D_MODEL)

            def ns(m):
                A = m @ m.T
                Bm = 1.5 * jnp.eye(HEAD_DIM, dtype=m.dtype) - 0.5 * A
                return Bm @ m
            return jax.vmap(ns)(chunks).reshape(w.shape)
        key = jax.random.key(seed)
        ks = jax.random.split(key, 6)

        def lin(k, out_dim, in_dim):
            bound = 1.0 / np.sqrt(in_dim)
            return jax.random.uniform(k, (out_dim, in_dim), jnp.float32, -bound, bound)
        Wq = _orthogonalize_per_head(lin(ks[0], N_HEADS * HEAD_DIM, D_MODEL))
        return {'x': jax.random.normal(ks[1], (B, T, D_MODEL), jnp.float32), 'Wq': Wq, 'Wkv_down': lin(ks[2], KV_LRANK, D_MODEL), 'Wk_up': lin(ks[3], N_HEADS * HEAD_DIM, KV_LRANK), 'Wv_up': lin(ks[4], N_HEADS * HEAD_DIM, KV_LRANK), 'Wo': lin(ks[5], D_MODEL, N_HEADS * HEAD_DIM)}
    _L0_attn_in = _L0_attn_setup()

    def _L0_ffn_setup():
        import jax, jax.numpy as jnp
        import numpy as np
        B, S, H, I, E = (2, 1024, 256, 128, 8)
        key = jax.random.key(seed)
        ks = jax.random.split(key, 5)
        scale_h = 1.0 / np.sqrt(H)
        scale_i = 1.0 / np.sqrt(I)
        return {'hidden_states': jax.random.normal(ks[0], (B, S, H), dtype=jnp.float32), 'gate_w': jax.random.normal(ks[1], (E, H), dtype=jnp.float32) * scale_h, 'w_gate': jax.random.normal(ks[2], (E, I, H), dtype=jnp.float32) * scale_h, 'w_up': jax.random.normal(ks[3], (E, I, H), dtype=jnp.float32) * scale_h, 'w_down': jax.random.normal(ks[4], (E, H, I), dtype=jnp.float32) * scale_i}
    _L0_ffn_in = _L0_ffn_setup()
    _d = {'L0_attn_x': _L0_attn_in['x'], 'L0_attn_Wq': _L0_attn_in['Wq'], 'L0_attn_Wkv_down': _L0_attn_in['Wkv_down'], 'L0_attn_Wk_up': _L0_attn_in['Wk_up'], 'L0_attn_Wv_up': _L0_attn_in['Wv_up'], 'L0_attn_Wo': _L0_attn_in['Wo'], 'L0_ffn_gate_w': _L0_ffn_in['gate_w'], 'L0_ffn_w_gate': _L0_ffn_in['w_gate'], 'L0_ffn_w_up': _L0_ffn_in['w_up'], 'L0_ffn_w_down': _L0_ffn_in['w_down']}
    _x0 = _d['L0_attn_x']
    _d['L0_attn_x'] = jax.random.normal(jax.random.fold_in(jax.random.key(seed), 1), (4, 1024, 256), dtype=_x0.dtype)
    del _x0
    return _d

def reference(L0_attn_x, L0_attn_Wq, L0_attn_Wkv_down, L0_attn_Wk_up, L0_attn_Wv_up, L0_attn_Wo, L0_ffn_gate_w, L0_ffn_w_gate, L0_ffn_w_up, L0_ffn_w_down):

    def _L0_attn_ref(x, Wq, Wkv_down, Wk_up, Wv_up, Wo):
        import jax, jax.numpy as jnp
        import numpy as np
        B, T = (4, 512)
        D_MODEL = 256
        N_HEADS = 8
        HEAD_DIM = 64
        KV_LRANK = 64

        def _orthogonalize_per_head(w):
            chunks = w.reshape(N_HEADS, HEAD_DIM, D_MODEL)

            def ns(m):
                A = m @ m.T
                Bm = 1.5 * jnp.eye(HEAD_DIM, dtype=m.dtype) - 0.5 * A
                return Bm @ m
            return jax.vmap(ns)(chunks).reshape(w.shape)
        b, t, _ = x.shape
        q = (x @ Wq.T).reshape(b, t, N_HEADS, HEAD_DIM)
        kv_latent = x @ Wkv_down.T
        k = (kv_latent @ Wk_up.T).reshape(b, t, N_HEADS, HEAD_DIM)
        v = (kv_latent @ Wv_up.T).reshape(b, t, N_HEADS, HEAD_DIM)
        scale = HEAD_DIM ** (-0.5)
        scores = jnp.einsum('bqhd,bkhd->bhqk', q, k) * scale
        attn = jax.nn.softmax(scores, axis=-1)
        out = jnp.einsum('bhqk,bkhd->bqhd', attn, v)
        out = out.reshape(b, t, N_HEADS * HEAD_DIM)
        return out @ Wo.T

    def _L0_ffn_ref(hidden_states, gate_w, w_gate, w_up, w_down):
        import jax, jax.numpy as jnp
        import numpy as np
        B, S, H, I, E = (2, 1024, 256, 128, 8)
        b, s, h = hidden_states.shape
        x = hidden_states.reshape(-1, h)
        logits = x @ gate_w.T
        top_v = jnp.max(logits, axis=-1)
        sel = jnp.argmax(logits, axis=-1)
        rw = jax.nn.sigmoid(top_v)
        out = jnp.zeros_like(x)
        n_exp = gate_w.shape[0]
        for e in range(n_exp):
            mask = (sel == e).astype(x.dtype)
            xs = x * (rw * mask)[:, None]
            g = xs @ w_gate[e].T
            u = xs @ w_up[e].T
            out = out + u * jax.nn.silu(g) @ w_down[e].T
        return out.reshape(b, s, h)
    x = L0_attn_x
    x = x + 0.5 * _L0_ffn_ref(_layernorm(x, axis=-1), L0_ffn_gate_w, L0_ffn_w_gate, L0_ffn_w_up, L0_ffn_w_down)
    x = x + _L0_attn_ref(_layernorm(x, axis=-1), L0_attn_Wq, L0_attn_Wkv_down, L0_attn_Wk_up, L0_attn_Wv_up, L0_attn_Wo)
    x = x + 0.5 * _L0_ffn_ref(_layernorm(x, axis=-1), L0_ffn_gate_w, L0_ffn_w_gate, L0_ffn_w_up, L0_ffn_w_down)
    return x

_drawn_inputs = setup_inputs


def setup_inputs(seed=0):
    import zlib

    import numpy as np

    out = dict(_drawn_inputs(seed))
    spreads = {}
    factors = {'L0_attn_Wq': 3.989,
     'L0_attn_Wkv_down': 4.05,
     'L0_attn_Wk_up': 3.821,
     'L0_attn_Wv_up': 3.5,
     'L0_attn_Wo': 3.448}
    for name, (base, spread) in spreads.items():
        noise = np.random.default_rng([zlib.crc32(name.encode()), seed]).standard_normal(out[name].shape)
        drawn = base * np.exp(spread * noise) if base else spread * noise
        out[name] = jnp.asarray(drawn.astype(out[name].dtype))
    for name, factor in factors.items():
        out[name] = (out[name] * factor).astype(out[name].dtype)
    return out
```

```python
from contextlib import ExitStack

import concourse.bass as bass
from concourse import mybir
from concourse.alu_op_type import AluOpType as ALU

ACT = mybir.ActivationFunctionType
F32 = mybir.dt.float32
F32R = mybir.dt.float32r
I32 = mybir.dt.int32
AX_X = mybir.AxisListType.X
ds = bass.ds

P = 128
D = 256
DC = D // P
BATCH = 4
SEQ = 1024
TOK = BATCH * SEQ
NT = TOK // P
HEADS = 8
HD = 64
PAIRS = HEADS // 2
EXPERTS = 8
INNER = 128
SLOT_TILES = NT + EXPERTS
SLOTS = SLOT_TILES * P
EPS = 1e-5
SCALE = HD ** -0.5
HALF = 512
QT = SEQ // P
KT = SEQ // P
STEPS = 2 * KT
MAXES = 2 * QT * 2
RING = 4
A_STEPS = (5, 7)


def build(nc, x_in, gate_t, w_gu, w_dn, w_q, w_k, w_v, w_o_t, w_kvd, out):
    with ExitStack() as ctx:
        def sb(name, shape, dt=F32):
            return ctx.enter_context(nc.sbuf_tensor(name, shape, dt))

        sems = {}

        def sem(name):
            if name not in sems:
                sems[name] = ctx.enter_context(nc.semaphore(name))
            return sems[name]

        sorted_x = nc.dram_tensor("sorted_x", [SLOTS, D], F32, kind="Internal").ap()
        sorted_y = nc.dram_tensor("sorted_y", [SLOTS, D], F32, kind="Internal").ap()

        x_res = sb("x_res", [P, NT * D])
        arena_a = sb("arena_a", [P, DC * TOK])
        arena_b = sb("arena_b", [P, 8192])
        keys = sb("keys", [P, 2, TOK], F32R)
        keys_now = sb("keys_now", [P, 2, SEQ], F32R)
        latent = sb("latent", [P, NT, HD])
        latent_now = sb("latent_now", [P, KT, HD])
        q_split = sb("q_split", [P, PAIRS, 2, SEQ], F32R)
        q_shift = sb("q_shift", [P, 2, 2, SEQ], F32R)
        w_qk = sb("w_qk", [P, DC, PAIRS, P])
        w_vo = sb("w_vo", [P, PAIRS, D])
        ident = sb("ident", [P, P])
        before = sb("before", [P, P])
        ones = sb("ones", [P, P])
        gate_w = sb("gate_w", [P, DC, EXPERTS])
        kvd = sb("kvd", [P, DC, P])
        stats = sb("stats", [P, NT, 6])
        st = sb("st", [P, 8, NT])
        slots = sb("slots", [P, NT], I32)
        slot_now = sb("slot_now", [P, RING], I32)
        tile_expert = sb("tile_expert", [P, SLOT_TILES], I32)
        small = sb("small", [P, 8, EXPERTS])
        small_i = sb("small_i", [P, EXPERTS], I32)
        eps_col = sb("eps_col", [P, 1])
        maxes = sb("maxes", [P, MAXES])
        top_q = sb("top_q", [P, 2 * QT])
        shift_q = sb("shift_q", [P, 4 * QT])
        shift_t = sb("shift_t", [4 * QT, P], F32R)
        denom = sb("denom", [P, 2, 4])
        inv_denom = sb("inv_denom", [P, 2, 4])

        xn_t = arena_a[:, :].rearrange("p (c n) -> p c n", c=DC)
        gu_sb = arena_a[:, 0:4096].rearrange("p (e c n) -> p e c n", e=EXPERTS, c=DC)
        dn_sb = arena_a[:, 4096:6144].rearrange("p (e n) -> p e n", e=EXPERTS)

        def route_tmp(n):
            return arena_a[:, 6144 + n * 256:6144 + (n + 1) * 256].rearrange("p (t e) -> p t e", e=EXPERTS)

        att_o = arena_b[:, 0:4096].rearrange("p (h n) -> p h n", h=PAIRS)
        prob = arena_b[:, 4096:6144].rearrange("p (b a n) -> p b a n", b=2, a=2)
        prob_sum = arena_b[:, 6144:8192].rearrange("p (b a n) -> p b a n", b=2, a=2)
        take_at = [0]

        def take(n, w):
            a = take_at[0]
            take_at[0] += n * w
            return arena_b[:, a:a + n * w].rearrange("p (b n) -> p b n", b=n)

        q_raw, k_raw, v_raw, o_raw = take(PAIRS, D), take(PAIRS, HD), take(PAIRS, HD), take(PAIRS, D)
        x_row = take(2, D)
        x_col = take(2, D)
        rows_out = take(RING, D)
        rows_in = take(RING, D)
        rows_t = take(2, D)
        silu_g = take(2, INNER)
        hid = take(2, INNER)
        hid_t = take(2, INNER)
        y_rows = take(RING, D)
        zeros = y_rows[:, 0, :]
        lat_f = arena_b[:, 4096:4096 + HALF]
        assert take_at[0] <= 8192

        ps = [ctx.enter_context(nc.psum_tensor(f"ps{i}", [P, 2, HALF], F32)) for i in range(3)]
        ps_o = ctx.enter_context(nc.psum_tensor("ps_o", [P, HALF], F32))
        ps_x = ctx.enter_context(nc.psum_tensor("ps_x", [P, HALF], F32))
        banks = [ps[i][:, j, :] for i in range(3) for j in range(2)] + [ps_o[:, :], ps_x[:, :]]
        ps_s = ps[0:2]
        ps_m = [ps[2][:, j, :] for j in range(2)]

        x_tiles = x_in.rearrange("b (t p) d -> p (b t) d", p=P)
        out_tiles = out.rearrange("b (t p) d -> p (b t) d", p=P)

        def x_tile(t):
            return x_res[:, ds(t * D, D)] if not isinstance(t, int) else x_res[:, t * D:(t + 1) * D]

        def each(eng, n, body):
            body(0, True)
            with eng.Fori(1, n) as i:
                body(i, False)

        block = ctx.enter_context(nc.Block())


        def pe_transposed(pe, tag, logits):
            def body(i, first):
                for k in range(2):
                    t = 2 * i + k
                    pe.wait_ge(sem(f"row_ready_{tag}"), t + 1)
                    if not first:
                        pe.wait_ge(sem(f"col_ready_{tag}"), t - 1)
                    for c in range(DC):
                        last = nc.tensor.transpose(banks[k][:, c * P:(c + 1) * P],
                                                   x_row[:, k, c * P:(c + 1) * P], ident[:, :])
                    last.then_inc(sem(f"row_turned_{tag}"), 1)
                if logits:
                    for k in range(2):
                        t = 2 * i + k
                        pe.wait_ge(sem(f"col_ready_{tag}"), t + 1)
                        for c in range(DC):
                            last = nc.tensor.matmul(banks[2][:, ds(t * EXPERTS, EXPERTS)],
                                                    x_col[:, k, c * P:(c + 1) * P], gate_w[:, c, :],
                                                    start=(c == 0), stop=(c == DC - 1))
                        last.then_inc(sem(f"logit_{tag}"), 1)
            each(pe, NT // 2, body)

        def act_transposed(act, tag, logits):
            def body(i, first):
                for k in range(2):
                    t = 2 * i + k
                    act.wait_ge(sem(f"row_turned_{tag}"), t + 1)
                    if logits:
                        if not first:
                            act.wait_ge(sem(f"logit_{tag}"), t - 1)
                        nc.scalar.activation(x_col[:, k, :], banks[k][:, 0:D], ACT.Copy) \
                            .then_inc(sem(f"col_ready_{tag}"), 1)
                    else:
                        nc.scalar.activation(xn_t[:, :, ds(t * P, P)],
                                             banks[k][:, 0:D].rearrange("p (c n) -> p c n", c=DC), ACT.Copy) \
                            .then_inc(sem(f"col_ready_{tag}"), 1)
            each(act, NT // 2, body)

        def dve_rows(dve, tag):
            def body(i, first):
                for k in range(2):
                    t = 2 * i + k
                    if not first:
                        dve.wait_ge(sem(f"row_turned_{tag}"), t - 1)
                    nc.vector.tensor_scalar(x_row[:, k, :], x_tile(t), st[:, 4, ds(t, 1)], st[:, 5, ds(t, 1)],
                                            ALU.mult, ALU.add).then_inc(sem(f"row_ready_{tag}"), 1)
            each(dve, NT // 2, body)

        link_count = [0]

        def link(ins):
            link_count[0] += 1
            ins.then_inc(sem("dve_link"), 1)
            nc.vector.wait_ge(sem("dve_link"), link_count[0])

        def dve_stats(dve, tag):
            with dve.Fori(0, NT) as t:
                if tag == "f1":
                    dve.wait_ge(sem("x_loaded"), 16 * NT)
                nc.vector.bn_stats(stats[:, ds(t, 1), :], x_tile(t)).then_inc(sem(f"stats_{tag}"), 1)
            dve.wait_ge(sem(f"stats_{tag}"), NT)
            nc.vector.tensor_tensor(st[:, 0, :], stats[:, :, 1], stats[:, :, 4], ALU.add)
            link(nc.vector.tensor_tensor(st[:, 1, :], stats[:, :, 1], stats[:, :, 4], ALU.subtract))
            nc.vector.tensor_tensor(st[:, 2, :], stats[:, :, 2], stats[:, :, 5], ALU.add)
            link(nc.vector.tensor_tensor(st[:, 1, :], st[:, 1, :], st[:, 1, :], ALU.mult))
            link(nc.vector.tensor_scalar(st[:, 2, :], st[:, 2, :], 1.0 / D, EPS, ALU.mult, ALU.add))
            link(nc.vector.scalar_tensor_tensor(st[:, 2, :], st[:, 1, :], 0.25, st[:, 2, :], ALU.mult, ALU.add))
            nc.vector.tensor_copy(st[:, 1, :], st[:, 2, :]).then_inc(sem(f"var_{tag}"), 1)
            dve.wait_ge(sem(f"std_{tag}"), 1)
            link(nc.vector.reciprocal(st[:, 4, :], st[:, 3, :]))
            link(nc.vector.tensor_tensor(st[:, 1, :], st[:, 4, :], st[:, 4, :], ALU.mult))
            link(nc.vector.tensor_tensor(st[:, 1, :], st[:, 1, :], st[:, 2, :], ALU.mult))
            link(nc.vector.tensor_scalar(st[:, 1, :], st[:, 1, :], -0.5, 1.5, ALU.mult, ALU.add))
            link(nc.vector.tensor_tensor(st[:, 4, :], st[:, 4, :], st[:, 1, :], ALU.mult))
            link(nc.vector.scalar_tensor_tensor(st[:, 5, :], st[:, 0, :], -0.5, st[:, 4, :], ALU.mult, ALU.mult))

        def act_std(act, tag):
            act.wait_ge(sem(f"var_{tag}"), 1)
            nc.scalar.activation(st[:, 3, :], st[:, 1, :], ACT.Sqrt).then_inc(sem(f"std_{tag}"), 1)


        def dve_route(dve, tag):
            top, rank, one_hot = st[:, 6, :], route_tmp(1), route_tmp(2)
            wide = [P, NT, EXPERTS]
            dve.wait_ge(sem(f"logit_{tag}"), NT)
            lg = banks[2][:, 0:NT * EXPERTS].rearrange("p (t e) -> p t e", e=EXPERTS)
            link(nc.vector.tensor_reduce(top, lg, AX_X, ALU.max))
            nc.vector.tensor_copy(st[:, 7, :], top).then_inc(sem(f"top_{tag}"), 1)
            link(nc.vector.tensor_tensor(rank, lg, top.unsqueeze(2).to_broadcast(wide), ALU.is_equal))
            link(nc.vector.tensor_tensor(rank, rank, small[:, 7, :].unsqueeze(1).to_broadcast(wide), ALU.mult))
            link(nc.vector.tensor_reduce(top, rank, AX_X, ALU.max))
            link(nc.vector.tensor_tensor(one_hot, rank, top.unsqueeze(2).to_broadcast(wide), ALU.is_equal))
            nc.vector.tensor_copy(route_tmp(0), one_hot).then_inc(sem(f"one_hot_{tag}"), 1)
            dve.wait_ge(sem(f"exp_top_{tag}"), 1)
            link(nc.vector.tensor_scalar(st[:, 3, :], st[:, 3, :], 1.0, None, ALU.add))
            link(nc.vector.reciprocal(st[:, 3, :], st[:, 3, :]))
            nc.vector.tensor_tensor(st[:, 4, :], st[:, 4, :], st[:, 3, :], ALU.mult)
            link(nc.vector.tensor_tensor(st[:, 5, :], st[:, 5, :], st[:, 3, :], ALU.mult))
            dve.wait_ge(sem(f"ranks_{tag}"), 2)
            a, b = route_tmp(0), route_tmp(3)
            counts = banks[4][:, 0:NT * EXPERTS].rearrange("p (t e) -> p t e", e=EXPERTS)
            link(nc.vector.tensor_copy(a, counts))
            s = 1
            while s < NT:
                nc.vector.tensor_copy(b[:, 0:s, :], a[:, 0:s, :])
                link(nc.vector.tensor_tensor(b[:, s:NT, :], a[:, s:NT, :], a[:, 0:NT - s, :], ALU.add))
                a, b = b, a
                s *= 2
            n, up, end, base, tmp = (small[:, j, :] for j in range(5))
            link(nc.vector.tensor_scalar(n, a[:, NT - 1, :], float(P - 1), None, ALU.add))
            link(nc.vector.tensor_copy(small_i[:, :], n))
            link(nc.vector.tensor_scalar(small_i[:, :], small_i[:, :], 7, 7, ALU.logical_shift_right,
                                         ALU.logical_shift_left))
            link(nc.vector.tensor_copy(up, small_i[:, :]))
            link(nc.vector.tensor_copy(end, up))
            s, u, v = 1, end, tmp
            while s < EXPERTS:
                nc.vector.tensor_copy(v[:, 0:s], u[:, 0:s])
                link(nc.vector.tensor_tensor(v[:, s:EXPERTS], u[:, s:EXPERTS], u[:, 0:EXPERTS - s], ALU.add))
                u, v = v, u
                s *= 2
            link(nc.vector.tensor_tensor(base, u, up, ALU.subtract))
            within = banks[3][:, 0:NT * EXPERTS].rearrange("p (t e) -> p t e", e=EXPERTS)
            link(nc.vector.tensor_tensor(a, a, counts, ALU.subtract))
            link(nc.vector.tensor_tensor(a, a, within, ALU.add))
            link(nc.vector.tensor_tensor(a, a, base.unsqueeze(1).to_broadcast(wide), ALU.add))
            link(nc.vector.tensor_tensor(a, a, one_hot, ALU.mult))
            link(nc.vector.tensor_reduce(top, a, AX_X, ALU.add))
            nc.vector.tensor_copy(slots[:, :], top)
            tiles = [P, SLOT_TILES, EXPERTS]
            cmp_a = arena_a[:, 6144 + 1024:6144 + 1024 + SLOT_TILES * EXPERTS].rearrange("p (t e) -> p t e", e=EXPERTS)
            row0 = arena_a[:, 6144 + 1400:6144 + 1400 + SLOT_TILES]
            cnt = arena_a[:, 6144 + 1450:6144 + 1450 + SLOT_TILES]
            dve.wait_ge(sem(f"row0_{tag}"), 1)
            link(nc.vector.tensor_tensor(cmp_a, u.unsqueeze(1).to_broadcast(tiles),
                                         row0.unsqueeze(2).to_broadcast(tiles), ALU.is_le))
            link(nc.vector.tensor_reduce(cnt, cmp_a, AX_X, ALU.add))
            link(nc.vector.tensor_scalar(cnt, cnt, float(EXPERTS - 1), None, ALU.min))
            nc.vector.tensor_copy(tile_expert[:, :], cnt).then_inc(sem(f"tile_expert_{tag}"), 1)
            dve.wait_ge(sem(f"tile_expert_{tag}"), 1)

        def pool_row0(pool, tag):
            row0 = arena_a[:, 6144 + 1400:6144 + 1400 + SLOT_TILES]
            pool.iota(row0, [[P, SLOT_TILES]], base=0, channel_multiplier=0,
                      allow_small_or_imprecise_dtypes=True).then_inc(sem(f"row0_{tag}"), 1)

        def pe_ranks(pe, tag):
            pe.wait_ge(sem(f"one_hot_{tag}"), 1)
            hot = route_tmp(0).rearrange("p t e -> p (t e)")
            nc.tensor.matmul(banks[3][:, 0:NT * EXPERTS], before[:, :], hot, start=True, stop=True) \
                .then_inc(sem(f"ranks_{tag}"), 1)
            nc.tensor.matmul(banks[4][:, 0:NT * EXPERTS], ones[:, :], hot, start=True, stop=True) \
                .then_inc(sem(f"ranks_{tag}"), 1)

        def act_exp_top(act, tag):
            act.wait_ge(sem(f"top_{tag}"), 1)
            nc.scalar.activation(st[:, 3, :], st[:, 7, :], ACT.Exp, scale=-1.0).then_inc(sem(f"exp_top_{tag}"), 1)

        def dve_scatter(dve, tag):
            def body(i, first):
                for k in range(RING):
                    t = RING * i + k
                    if not first:
                        dve.wait_ge(sem(f"scattered{k}_{tag}"), 16 * i)
                    nc.vector.tensor_copy(slot_now[:, k:k + 1], slots[:, ds(t, 1)]) \
                        .then_inc(sem(f"to_scatter_{tag}"), 1)
                    nc.vector.tensor_scalar(rows_out[:, k, :], x_tile(t), st[:, 4, ds(t, 1)], st[:, 5, ds(t, 1)],
                                            ALU.mult, ALU.add).then_inc(sem(f"to_scatter_{tag}"), 1)
            each(dve, NT // RING, body)

        def pool_scatter(pool, tag):
            pool.wait_ge(sem("zero_filled"), 16)
            for t in range(NT):
                k = t % RING
                pool.wait_ge(sem(f"to_scatter_{tag}"), 2 * (t + 1))
                pool.indirect_dma_start(sorted_x[:, :], bass.IndirectOffsetOnAxis(ap=slot_now[:, k:k + 1], axis=0),
                                        rows_out[:, k, :], None).then_inc(sem(f"scattered{k}_{tag}"), 16)

        def sp_experts(sp, tag):
            groups = SLOT_TILES // RING
            for k in range(RING):
                sp.wait_ge(sem(f"scattered{k}_{tag}"), 16 * (NT // RING))

            def load(i, first):
                for k in range(RING):
                    t = RING * i + k
                    row = t * P if first else sp.snap(t * P)
                    if not first:
                        sp.wait_ge(sem(f"in_turned_{tag}"), t - RING + 1)
                    sp.dma_start(rows_in[:, k, :], sorted_x[ds(row, P), :]).then_inc(sem(f"in{k}_{tag}"), 16)

            def store(i):
                for k in range(RING):
                    t = RING * i + k
                    row = t * P if isinstance(t, int) else sp.snap(t * P)
                    sp.wait_ge(sem(f"y_ready_{tag}"), t + 1)
                    sp.dma_start(sorted_y[ds(row, P), :], y_rows[:, k, :]).then_inc(sem(f"y_stored{k}_{tag}"), 16)
            load(0, True)
            with sp.Fori(1, groups) as i:
                load(i, False)
                store(i - 1)
            store(groups - 1)

        def pe_experts(pe, tag):
            def turn(t, k, start):
                pe.wait_ge(sem(f"in{k}_{tag}"), 16 * (t // RING + 1) if isinstance(t, int) else (t - k) * 4 + 16)
                if not start:
                    pe.wait_ge(sem(f"in_copied_{tag}"), t - 1)
                for c in range(DC):
                    last = nc.tensor.transpose(banks[k % 2][:, c * P:(c + 1) * P], rows_in[:, k, c * P:(c + 1) * P],
                                               ident[:, :])
                last.then_inc(sem(f"in_turned_{tag}"), 1)

            def expert(t):
                return pe.value_load(tile_expert[0:1, ds(t, 1)], min_val=0, max_val=EXPERTS - 1)

            def gate_up(t, k, start):
                e = expert(t)
                pe.wait_ge(sem(f"in_copied_{tag}"), t + 1)
                if not start:
                    pe.wait_ge(sem(f"hid_{tag}"), t - 1)
                for c in range(DC):
                    last = nc.tensor.matmul(banks[2 + k % 2][:, 0:2 * INNER], rows_t[:, k % 2, c * P:(c + 1) * P],
                                            arena_a[:, ds(e * (DC * 2 * INNER) + c * 2 * INNER, 2 * INNER)],
                                            start=(c == 0), stop=(c == DC - 1))
                last.then_inc(sem(f"gate_up_{tag}"), 1)

            def down(t, k, start):
                e = expert(t)
                pe.wait_ge(sem(f"hid_{tag}"), t + 1)
                if not start:
                    pe.wait_ge(sem(f"hid_copied_{tag}"), t - 1)
                nc.tensor.transpose(banks[4 + k % 2][:, 0:P], hid[:, k % 2, :], ident[:, :]) \
                    .then_inc(sem(f"hid_turned_{tag}"), 1)
                pe.wait_ge(sem(f"hid_copied_{tag}"), t + 1)
                if not start:
                    pe.wait_ge(sem(f"y_ready_{tag}"), t - 1)
                nc.tensor.matmul(banks[6 + k % 2][:, 0:D], hid_t[:, k % 2, :], arena_a[:, ds(e * D + 4096, D)],
                                 start=True, stop=True).then_inc(sem(f"down_{tag}"), 1)

            pe.wait_ge(sem(f"experts_loaded_{tag}"), 32)
            pe.wait_ge(sem(f"tile_expert_{tag}"), 1)

            def group(i, first, last):
                for k in range(RING):
                    t = RING * i + k
                    if not (last and k == RING - 1):
                        turn(t + 1, (k + 1) % RING, first and k == 0)
                    gate_up(t, k, first and k < 2)
                    if not (first and k == 0):
                        down(t - 1, (k - 1) % RING, first and k < 3)
            turn(0, 0, True)
            group(0, True, False)
            with pe.Fori(1, SLOT_TILES // RING - 1) as i:
                group(i, False, False)
            group(SLOT_TILES // RING - 1, False, True)
            down(SLOT_TILES - 1, RING - 1, False)

        def act_experts(act, tag):
            def copy_in(t, k, start):
                act.wait_ge(sem(f"in_turned_{tag}"), t + 1)
                if not start:
                    act.wait_ge(sem(f"gate_up_{tag}"), t - 1)
                nc.scalar.activation(rows_t[:, k % 2, :], banks[k % 2][:, 0:D], ACT.Copy) \
                    .then_inc(sem(f"in_copied_{tag}"), 1)

            def silu(t, k, start):
                act.wait_ge(sem(f"gate_up_{tag}"), t + 1)
                if not start:
                    act.wait_ge(sem(f"hid_{tag}"), t - 1)
                nc.scalar.activation(silu_g[:, k % 2, :], banks[2 + k % 2][:, 0:INNER], ACT.Silu) \
                    .then_inc(sem(f"silu_{tag}"), 1)

            def y_out(t, k, start):
                act.wait_ge(sem(f"down_{tag}"), t + 1)
                if not start:
                    act.wait_ge(sem(f"y_stored{k}_{tag}"), (t - k) * 4)
                nc.scalar.activation(y_rows[:, k, :], banks[6 + k % 2][:, 0:D], ACT.Copy) \
                    .then_inc(sem(f"y_ready_{tag}"), 1)

            def group(i, first=False, second=False, last=False):
                for k in range(RING):
                    t = RING * i + k
                    if not (last and k == RING - 1):
                        copy_in(t + 1, (k + 1) % RING, first and k == 0)
                    silu(t, k, first and k < 2)
                    if not (first and k == 0):
                        y_out(t - 1, (k - 1) % RING, first or second and k == 0)
            copy_in(0, 0, True)
            group(0, first=True)
            group(1, second=True)
            with act.Fori(2, SLOT_TILES // RING - 1) as i:
                group(i)
            group(SLOT_TILES // RING - 1, last=True)
            y_out(SLOT_TILES - 1, RING - 1, False)

        def dve_experts(dve, tag):
            def copy_hid(t, k, start):
                dve.wait_ge(sem(f"hid_turned_{tag}"), t + 1)
                if not start:
                    dve.wait_ge(sem(f"down_{tag}"), t - 1)
                nc.vector.tensor_copy(hid_t[:, k % 2, :], banks[4 + k % 2][:, 0:P]) \
                    .then_inc(sem(f"hid_copied_{tag}"), 1)

            def gated(t, k, start):
                dve.wait_ge(sem(f"silu_{tag}"), t + 1)
                if not start:
                    dve.wait_ge(sem(f"hid_turned_{tag}"), t - 1)
                nc.vector.tensor_tensor(hid[:, k % 2, :], silu_g[:, k % 2, :], banks[2 + k % 2][:, INNER:2 * INNER],
                                        ALU.mult).then_inc(sem(f"hid_{tag}"), 1)

            def body(i, first):
                for k in range(RING):
                    t = RING * i + k
                    if not (first and k == 0):
                        copy_hid(t - 1, (k - 1) % RING, first and k < 3)
                    gated(t, k, first and k < 2)
            each(dve, SLOT_TILES // RING, body)
            copy_hid(SLOT_TILES - 1, RING - 1, False)

        def pool_gather(pool, tag):
            for k in range(RING):
                pool.wait_ge(sem(f"y_stored{k}_{tag}"), 16 * (SLOT_TILES // RING))
            for t in range(NT):
                k = t % RING
                pool.wait_ge(sem(f"slot_back_{tag}"), t + 1)
                pool.indirect_dma_start(rows_out[:, k, :], None, sorted_y[:, :],
                                        bass.IndirectOffsetOnAxis(ap=slot_now[:, k:k + 1], axis=0)) \
                    .then_inc(sem(f"gathered{k}_{tag}"), 16)

        def dve_gather(dve, tag):
            for k in range(RING):
                dve.wait_ge(sem(f"scattered{k}_{tag}"), 16 * (NT // RING))
                nc.vector.tensor_copy(slot_now[:, k:k + 1], slots[:, k:k + 1]).then_inc(sem(f"slot_back_{tag}"), 1)

            def body(i, last):
                for k in range(RING):
                    t = RING * i + k
                    dve.wait_ge(sem(f"gathered{k}_{tag}"), 16 * i + 16)
                    nc.vector.scalar_tensor_tensor(x_tile(t), rows_out[:, k, :], 0.5, x_tile(t),
                                                   ALU.mult, ALU.add).then_inc(sem(f"ffn_added_{tag}"), 1)
                    if not last:
                        dve.wait_ge(sem(f"ffn_added_{tag}"), t + 1)
                        nc.vector.tensor_copy(slot_now[:, k:k + 1], slots[:, ds(t + RING, 1)]) \
                            .then_inc(sem(f"slot_back_{tag}"), 1)
            with dve.Fori(0, NT // RING - 1) as i:
                body(i, False)
            body(NT // RING - 1, True)
            dve.wait_ge(sem(f"ffn_added_{tag}"), NT)


        def pe_queries(pe, slot, c, tokens, use):
            for d in range(DC):
                last = nc.tensor.matmul(ps_x[:, :], w_qk[:, d, slot, :], xn_t[:, d, ds(tokens, HALF)],
                                        start=(d == 0), stop=(d == DC - 1))
            last.then_inc(sem("q_made"), 1)

        def act_queries(act, slot, c, n):
            act.wait_ge(sem("q_made"), n + 1)
            for a in range(2):
                nc.scalar.activation(q_split[0:HD, slot, a, c * HALF:(c + 1) * HALF], ps_x[a * HD:(a + 1) * HD, :],
                                     ACT.Copy).then_inc(sem("q_hi"), 1)

        def dve_queries(dve, slot, c, n):
            for a in range(2):
                dve.wait_ge(sem("q_hi"), 2 * n + 2)
                nc.vector.tensor_tensor(q_split[HD:P, slot, a, c * HALF:(c + 1) * HALF], ps_x[a * HD:(a + 1) * HD, :],
                                        q_split[0:HD, slot, a, c * HALF:(c + 1) * HALF].bitcast(F32), ALU.subtract) \
                    .then_inc(sem("q_lo"), 1)

        def pe_max(pe, slot, m, key0, n, first):
            a, qt, half = m // (2 * QT), m // 2 % QT, m % 2
            if not first:
                pe.wait_ge(sem("max_taken"), n - 1)
            nc.tensor.matmul(ps_m[m % 2], q_split[:, slot, a, qt * P:(qt + 1) * P],
                             keys[:, 0, ds(key0 + half * HALF, HALF)], start=True, stop=True) \
                .then_inc(sem("max_scores"), 1)

        def dve_max(dve, m, n):
            dve.wait_ge(sem("max_scores"), n + 1)
            nc.vector.tensor_reduce(maxes[:, m:m + 1], ps_m[m % 2], AX_X, ALU.max).then_inc(sem("max_taken"), 1)

        def dve_shift(dve, n, u):
            dve.wait_ge(sem("max_taken"), n)
            pairs = maxes[:, :].rearrange("p (q h) -> p q h", h=2)
            hi = shift_q[:, :].rearrange("p (a s q) -> p a s q", a=2, s=2)
            nc.vector.tensor_tensor(top_q[:, :], pairs[:, :, 0], pairs[:, :, 1], ALU.max) \
                .then_inc(sem("shift_top"), 1)
            dve.wait_ge(sem("shift_top"), u + 1)
            top = top_q[:, :].rearrange("p (a q) -> p a q", a=2)
            if not isinstance(u, int) or u > 0:
                dve.wait_ge(sem("shift_turned"), u)
            nc.vector.tensor_scalar(hi[:, :, 0, :].bitcast(F32R), top, -1.0, None, ALU.mult) \
                .then_inc(sem("shift_hi"), 1)
            dve.wait_ge(sem("shift_hi"), u + 1)
            nc.vector.scalar_tensor_tensor(hi[:, :, 1, :].bitcast(F32R), top, -1.0, hi[:, :, 0, :],
                                           ALU.mult, ALU.subtract).then_inc(sem("shift_lo"), 1)

        def pe_shift(pe, u):
            pe.wait_ge(sem("shift_lo"), u + 1)
            nc.tensor.transpose(ps_x[0:4 * QT, 0:P], shift_q[:, :], ident[:, :]).then_inc(sem("shift_turned"), 1)

        def act_shift(act, u, b=None, p=None):
            act.wait_ge(sem("shift_turned"), u + 1)
            if b is not None:
                act.wait_ge(sem(f"shift_placed{p % 2}"), 32 * (2 * b + p // 2 + 1))
            nc.scalar.activation(shift_t[:, :], ps_x[0:4 * QT, 0:P], ACT.Copy).then_inc(sem("shift_copied"), 1)

        def sp_shift(sp, slot, u):
            sp.wait_ge(sem("shift_copied"), u + 1)
            for a in range(2):
                sp.dma_start(q_shift[HD:HD + 2, slot % 2, a, :].bitcast(F32),
                             shift_t[2 * QT * a:2 * QT * (a + 1), :].bitcast(F32)).then_inc(sem(f"shift_placed{slot % 2}"), 16)

        def sp_queries(sp, slot):
            sp.dma_start(q_shift[0:HD, slot % 2, :, :].bitcast(F32), q_split[0:HD, slot, :, :].bitcast(F32)).then_inc(sem(f"q_copied{slot % 2}"), 16)

        def pe_latents(pe):
            for j in range(TOK // HALF):
                if j >= 2:
                    pe.wait_ge(sem("lat_copied"), 3 * (j - 1))
                if j == 0:
                    pe.wait_ge(sem("col_ready_att"), NT)
                for d in range(DC):
                    last = nc.tensor.matmul(banks[2 + j % 2], kvd[:, d, :], xn_t[:, d, j * HALF:(j + 1) * HALF],
                                            start=(d == 0), stop=(d == DC - 1))
                last.then_inc(sem("lat_made"), 1)
                pe.wait_ge(sem("lat_f"), j + 1)
                if j >= 1:
                    pe.wait_ge(sem("lat_rows"), j)
                for g in range(4):
                    last = nc.tensor.transpose(banks[4][:, g * P:(g + 1) * P], lat_f[:, g * P:(g + 1) * P], ident[:, :])
                last.then_inc(sem("lat_turned"), 1)

        def act_latents(act):
            for j in range(TOK // HALF):
                act.wait_ge(sem("lat_made"), j + 1)
                if j >= 1:
                    act.wait_ge(sem("lat_turned"), j)
                nc.scalar.activation(lat_f, banks[2 + j % 2], ACT.Copy).then_inc(sem("lat_f"), 1)
                nc.scalar.activation(keys[:, 0, j * HALF:(j + 1) * HALF], banks[2 + j % 2], ACT.Copy) \
                    .then_inc(sem("lat_hi"), 1)

        def dve_latents(dve):
            for j in range(TOK // HALF):
                cols = slice(j * HALF, (j + 1) * HALF)
                dve.wait_ge(sem("lat_hi"), j + 1)
                nc.vector.tensor_tensor(keys[0:HD, 1, cols], banks[2 + j % 2][0:HD, :],
                                        keys[0:HD, 0, cols].bitcast(F32), ALU.subtract).then_inc(sem("lat_copied"), 3)
                dve.wait_ge(sem("lat_turned"), j + 1)
                nc.vector.tensor_copy(latent[:, 4 * j:4 * j + 4, :],
                                      banks[4].rearrange("p (g n) -> p g n", g=4)[:, :, 0:HD]) \
                    .then_inc(sem("lat_rows"), 1)

        STEP_B = PAIRS * STEPS
        SUM_B = PAIRS * 2 * (KT - 1)

        def pe_attention(pe):
            pe.wait_ge(sem("lat_rows"), TOK // HALF)
            pe.wait_ge(sem("lat_copied"), 3 * TOK // HALF)
            for n in range(4):
                if n:
                    pe.wait_ge(sem("q_lo"), 2 * n)
                pe_queries(pe, n // 2, n % 2, (n % 2) * HALF, n)
            pe.wait_ge(sem("q_lo"), 8)
            for m in range(MAXES):
                pe_max(pe, 0, m, 0, m, m < 2)
            pe_shift(pe, 0)
            pe.wait_ge(sem("batch_ready"), 48)
            pe.wait_ge(sem("keys_fill"), 1)
            pe.wait_ge(sem("q_fill"), 1)

            with pe.Fori(0, BATCH) as b:
                bn = (b + 1) % BATCH

                def scores(p, s):
                    c, kt = s // KT, s % KT
                    n = p * STEPS + s
                    if n == 0:
                        pe.wait_ge(sem("batch_ready"), 48 * b + 48)
                    if n >= 2:
                        pe.wait_ge(sem("exp_done"), STEP_B * b + n - 1)
                    if s == 0:
                        pe.wait_ge(sem(f"q_copied{p % 2}"), 16 * (2 * b + p // 2 + 1))
                        pe.wait_ge(sem(f"shift_placed{p % 2}"), 32 * (2 * b + p // 2 + 1))
                    for a in range(2):
                        o = ps_s[n % 2][:, a, :]
                        q = slice(c * HALF, (c + 1) * HALF)
                        k = slice(kt * P, (kt + 1) * P)
                        nc.tensor.matmul(o, keys_now[:, 0, k], q_split[:, p, a, q], start=True, stop=False)
                        last = nc.tensor.matmul(o, keys_now[:, 1, k], q_shift[:, p % 2, a, q], start=False, stop=True)
                    last.then_inc(sem("scored"), 1)

                def values(p, s):
                    c, kt = s // KT, s % KT
                    n = p * STEPS + s
                    pe.wait_ge(sem("exp_done"), STEP_B * b + n + 1)
                    if kt == 0 and p + c:
                        pe.wait_ge(sem("o_copied"), 2 * PAIRS * b + 2 * p + c)
                    for a in range(2):
                        src = prob_sum[:, c, a, :] if kt == 0 else prob[:, kt % 2, a, :]
                        last = nc.tensor.matmul(ps_o[a * HD:(a + 1) * HD, :], latent_now[:, kt, :], src,
                                                start=(kt == 0), stop=(kt == KT - 1))
                    last.then_inc(sem("valued"), 1)

                def turn_sum(p, c, a):
                    if a == 0:
                        pe.wait_ge(sem("summed"), SUM_B * b + (2 * p + c + 1) * (KT - 1))
                    if p + c + a:
                        pe.wait_ge(sem("denom"), 4 * PAIRS * b + 4 * p + 2 * c + a)
                    for g in range(4):
                        last = nc.tensor.transpose(ps_x[:, g * P:(g + 1) * P],
                                                   prob_sum[:, c, a, g * P:(g + 1) * P], ident[:, :])
                    last.then_inc(sem("sum_turned"), 1)

                def spread(p, c):
                    pe.wait_ge(sem("inv_denom"), 2 * PAIRS * b + 2 * p + c + 1)
                    for g in range(4):
                        for a in range(2):
                            last = nc.tensor.matmul(ps_x[a * HD:(a + 1) * HD, g * P:(g + 1) * P],
                                                    inv_denom[:, a, g:g + 1].to_broadcast([P, HD]), ident[:, :],
                                                    start=True, stop=True)
                    last.then_inc(sem("spread"), 1)

                for p in range(PAIRS):
                    wrap_m, wrap_a = p == PAIRS - 1, p >= PAIRS - 2
                    for s in range(STEPS):
                        scores(p, s)
                        if p or s:
                            values(p - (s == 0), (s - 1) % STEPS)
                        for m in range(3 * s, min(3 * s + 3, MAXES)):
                            if m == 0:
                                pe.wait_ge(sem("q_lo"), 4 * PAIRS * b + 4 * (p + 1) + 4)
                            pe_max(pe, (p + 1) % PAIRS, m, (bn if wrap_m else b) * SEQ,
                                   MAXES * PAIRS * b + MAXES * (p + 1) + m, False)
                        if p and s in (2, 3):
                            turn_sum(p - 1, 1, s - 2)
                        if p and s == 4:
                            spread(p - 1, 1)
                        if s in A_STEPS:
                            c = A_STEPS.index(s)
                            n = 2 * PAIRS * b + 2 * (p + 2) + c
                            pe.wait_ge(sem("q_lo"), 2 * n)
                            if p:
                                pe.wait_ge(sem("normed"), 2 * PAIRS * b + 2 * p)
                            pe_queries(pe, (p + 2) % PAIRS, c, (bn if wrap_a else b) * SEQ + c * HALF, n)
                        if s in (10, 11):
                            if s == 10:
                                pe.wait_ge(sem("q_lo"), 4 * PAIRS * b + 4 * (p + 3))
                            turn_sum(p, 0, s - 10)
                        if s == 12:
                            spread(p, 0)
                        if s == 14:
                            pe.wait_ge(sem("normed"), 2 * PAIRS * b + 2 * p + 1)
                            pe_shift(pe, PAIRS * b + p + 1)
                values(PAIRS - 1, STEPS - 1)
                pe.wait_ge(sem("shift_copied"), PAIRS * b + PAIRS + 1)
                turn_sum(PAIRS - 1, 1, 0)
                turn_sum(PAIRS - 1, 1, 1)
                spread(PAIRS - 1, 1)
                pe.wait_ge(sem("normed"), 2 * PAIRS * b + 2 * PAIRS)
                for t in range(QT):
                    if t >= 2:
                        pe.wait_ge(sem("att_added"), QT * b + t - 1)
                    else:
                        pe.wait_ge(sem("max_taken"), MAXES * PAIRS * b + MAXES * (PAIRS + 1))
                    for p in range(PAIRS):
                        last = nc.tensor.matmul(ps_m[t % 2][:, 0:D], att_o[:, p, t * P:(t + 1) * P], w_vo[:, p, :],
                                                start=(p == 0), stop=(p == PAIRS - 1))
                    last.then_inc(sem("projected"), 1)
                pe.wait_ge(sem("att_added"), QT * b + QT)

        def act_attention(act):
            for n in range(4):
                act_queries(act, n // 2, n % 2, n)
            act_shift(act, 0)
            with act.Fori(0, BATCH) as b:
                def exps(p, s):
                    c, kt = s // KT, s % KT
                    n = p * STEPS + s
                    act.wait_ge(sem("scored"), STEP_B * b + n + 1)
                    k = 2 * p + c
                    if kt == 0:
                        if p:
                            act.wait_ge(sem("sum_turned"), 4 * PAIRS * b + 4 * (p - 1) + 2 * c + 2)
                    else:
                        g = k * (KT - 1) + kt - 1
                        used_sum = g - (1 if kt == 1 else 3 if kt == 2 else 2)
                        used_val = n - (2 if kt >= 3 else 2 if kt == 1 else 4)
                        if used_sum >= 0:
                            act.wait_ge(sem("summed"), SUM_B * b + used_sum + 1)
                            act.wait_ge(sem("valued"), STEP_B * b + used_val + 1)
                    dst = prob_sum[:, c, :, :] if kt == 0 else prob[:, kt % 2, :, :]
                    nc.scalar.activation(dst, ps_s[n % 2][:, :, :], ACT.Exp, scale=SCALE).then_inc(sem("exp_done"), 1)

                def copy_o(p, c):
                    act.wait_ge(sem("valued"), STEP_B * b + p * STEPS + (c + 1) * KT)
                    nc.scalar.activation(att_o[:, p, c * HALF:(c + 1) * HALF], ps_o[:, :], ACT.Copy) \
                        .then_inc(sem("o_copied"), 1)

                for p in range(PAIRS):
                    for s in range(STEPS):
                        exps(p, s)
                        if s == 0 and p:
                            copy_o(p - 1, 1)
                        if s == KT:
                            copy_o(p, 0)
                        if s in A_STEPS:
                            c = A_STEPS.index(s)
                            act_queries(act, (p + 2) % PAIRS, c, 2 * PAIRS * b + 2 * (p + 2) + c)
                        if s == 14:
                            act_shift(act, PAIRS * b + p + 1, b, p)
                copy_o(PAIRS - 1, 1)

        def dve_attention(dve):
            for n in range(4):
                dve_queries(dve, n // 2, n % 2, n)
            for m in range(MAXES):
                dve_max(dve, m, m)
            dve_shift(dve, MAXES, 0)
            with dve.Fori(0, BATCH) as b:
                def denoms(p, c, a):
                    n = 4 * PAIRS * b + 4 * p + 2 * c + a
                    dve.wait_ge(sem("sum_turned"), n + 1)
                    if a == 0 and p + c:
                        dve.wait_ge(sem("inv_denom"), 2 * PAIRS * b + 2 * p + c)
                    nc.vector.tensor_reduce(denom[:, a, :], ps_x[:, :].rearrange("p (g n) -> p g n", g=4), AX_X,
                                            ALU.add).then_inc(sem("denom"), 1)
                    if a == 1:
                        dve.wait_ge(sem("denom"), n + 1)
                        if p + c:
                            dve.wait_ge(sem("spread"), 2 * PAIRS * b + 2 * p + c)
                        nc.vector.reciprocal(inv_denom[:, :, :], denom[:, :, :]).then_inc(sem("inv_denom"), 1)

                def norm(p, c):
                    dve.wait_ge(sem("spread"), 2 * PAIRS * b + 2 * p + c + 1)
                    dve.wait_ge(sem("o_copied"), 2 * PAIRS * b + 2 * p + c + 1)
                    o = att_o[:, p, c * HALF:(c + 1) * HALF]
                    nc.vector.tensor_tensor(o, o, ps_x[:, :], ALU.mult).then_inc(sem("normed"), 1)

                for p in range(PAIRS):
                    for s in range(STEPS):
                        for m in range(3 * s, min(3 * s + 3, MAXES)):
                            dve_max(dve, m, MAXES * PAIRS * b + MAXES * (p + 1) + m)
                        if p and s in (2, 3):
                            denoms(p - 1, 1, s - 2)
                        if p and s == 4:
                            norm(p - 1, 1)
                        if s in A_STEPS:
                            c = A_STEPS.index(s)
                            dve_queries(dve, (p + 2) % PAIRS, c, 2 * PAIRS * b + 2 * (p + 2) + c)
                        if s in (10, 11):
                            denoms(p, 0, s - 10)
                        if s == 12:
                            norm(p, 0)
                            dve_shift(dve, MAXES * PAIRS * b + MAXES * (p + 2), PAIRS * b + p + 1)
                denoms(PAIRS - 1, 1, 0)
                denoms(PAIRS - 1, 1, 1)
                norm(PAIRS - 1, 1)
                for t in range(QT):
                    dve.wait_ge(sem("projected"), QT * b + t + 1)
                    x = x_res[:, ds((b * QT + t) * D, D)]
                    nc.vector.tensor_tensor(x, x, ps_m[t % 2][:, 0:D], ALU.add).then_inc(sem("att_added"), 1)
            dve.wait_ge(sem("att_added"), NT)

        def pool_attention(pool):
            with pool.Fori(0, BATCH) as b:
                for p in range(PAIRS):
                    for c in range(2):
                        for kt in range(1, KT):
                            n = p * STEPS + c * KT + kt
                            k = 2 * p + c
                            pool.wait_ge(sem("exp_done"), STEP_B * b + n + 1)
                            if kt == 1:
                                pool.wait_ge(sem("valued"), STEP_B * b + n)
                            else:
                                pool.wait_ge(sem("summed"), SUM_B * b + k * (KT - 1) + kt - 1)
                            t = prob_sum[:, c, :, :].rearrange("p a n -> p (a n)")
                            nc.gpsimd.tensor_tensor(t, t, prob[:, kt % 2, :, :].rearrange("p a n -> p (a n)"), ALU.add) \
                                .then_inc(sem("summed"), 1)

        def sp_attention(sp):
            def batch(b, ready):
                key0, tile0 = (0, 0) if isinstance(b, int) else (sp.snap(b * SEQ), sp.snap(b * KT))
                ready()
                sp.dma_start(keys_now[:, 0, :].bitcast(F32), keys[:, 0, ds(key0, SEQ)].bitcast(F32)).then_inc(sem("batch_ready"), 16)
                sp.dma_start(keys_now[:, 1, :].bitcast(F32), keys[:, 1, ds(key0, SEQ)].bitcast(F32)).then_inc(sem("batch_ready"), 16)
                sp.dma_start(latent_now[:, :, :], latent[:, ds(tile0, KT), :]).then_inc(sem("batch_ready"), 16)
            sp.wait_ge(sem("lat_rows"), TOK // HALF)
            sp.wait_ge(sem("lat_copied"), 3 * TOK // HALF)
            sp.wait_ge(sem("keys_fill"), 1)
            batch(0, lambda: None)
            sp.wait_ge(sem("q_hi"), 8)
            sp.wait_ge(sem("q_fill"), 1)
            sp_queries(sp, 0)
            sp_shift(sp, 0, 0)
            with sp.Fori(0, BATCH) as b:
                for p in range(PAIRS):
                    if p:
                        sp.wait_ge(sem("scored"), STEP_B * b + STEPS * p)
                    sp_queries(sp, (p + 1) % PAIRS)
                    sp_shift(sp, (p + 1) % PAIRS, PAIRS * b + p + 1)

                def used_up():
                    sp.wait_ge(sem("valued"), STEP_B * b + STEP_B)
                batch((b + 1) % BATCH, used_up)
            sp.wait_ge(sem("batch_ready"), 48 * (BATCH + 1))
            for k in range(2):
                n = BATCH * PAIRS // 2 + 1 - k
                sp.wait_ge(sem(f"q_copied{k}"), 16 * n)
                sp.wait_ge(sem(f"shift_placed{k}"), 32 * n)


        @block.sync
        def _(sp):
            for t in range(NT):
                sp.dma_start(x_res[:, t * D:(t + 1) * D], x_tiles[:, t, :]).then_inc(sem("x_loaded"), 16)
            sp.dma_start(gate_w[:, :, :], gate_t).then_inc(sem("consts_loaded"), 16)
            for half in range(2):
                sp.dma_start(kvd[:, :, half * HD:(half + 1) * HD], w_kvd).then_inc(sem("consts_loaded"), 16)
            for dst, src in ((q_raw, w_q), (k_raw, w_k), (v_raw, w_v), (o_raw, w_o_t)):
                sp.dma_start(dst, src).then_inc(sem("raw_loaded"), 16)
            sp.wait_ge(sem("zeroed"), 1)
            sp.dma_start(sorted_x.rearrange("(n p) d -> p n d", p=P),
                         zeros.unsqueeze(1).to_broadcast([P, SLOT_TILES, D])).then_inc(sem("zero_filled"), 16)
            sp.dma_start(gu_sb, w_gu).then_inc(sem("experts_loaded_f1"), 16)
            sp.dma_start(dn_sb, w_dn).then_inc(sem("experts_loaded_f1"), 16)
            sp_experts(sp, "f1")
            sp_attention(sp)
            sp.wait_ge(sem("att_added"), NT)
            sp.dma_start(gu_sb, w_gu).then_inc(sem("experts_loaded_f2"), 16)
            sp.dma_start(dn_sb, w_dn).then_inc(sem("experts_loaded_f2"), 16)
            sp_experts(sp, "f2")
            with sp.Fori(0, NT) as t:
                col = sp.snap(t * D)
                sp.wait_ge(sem("ffn_added_f2"), t + 1)
                sp.dma_start(out_tiles[:, ds(t, 1), :], x_res[:, ds(col, D)].unsqueeze(1)) \
                    .then_inc(sem("out_stored"), 16)
            sp.wait_ge(sem("out_stored"), 16 * NT)

        @block.gpsimd
        def _(pool):
            def mask(dst, compare, name, fill, base):
                pool.affine_select(out=base, in_=base, pattern=[[-1, P]], compare_op=compare, fill=fill,
                                   base=0, channel_multiplier=1).then_inc(sem(name), 1)
            pool.memset(ones[:, :], 1.0).then_inc(sem("filled"), 1)
            pool.memset(ident[:, :], 0.0).then_inc(sem("filled"), 1)
            pool.memset(before[:, :], 0.0).then_inc(sem("filled"), 1)
            pool.wait_ge(sem("filled"), 3)
            mask(ident, ALU.not_equal, "masks", 1.0, ident[:, :])
            mask(before, ALU.is_ge, "masks", 1.0, before[:, :])
            pool.iota(small[:, 7, :], [[-1, EXPERTS]], base=EXPERTS, channel_multiplier=0,
                      allow_small_or_imprecise_dtypes=True).then_inc(sem("masks"), 1)
            pool_row0(pool, "f1")
            pool_scatter(pool, "f1")
            pool_gather(pool, "f1")
            pool_attention(pool)
            pool.wait_ge(sem("att_added"), NT)
            pool_row0(pool, "f2")
            pool_scatter(pool, "f2")
            pool_gather(pool, "f2")

        @block.vector
        def _(dve):
            nc.vector.memset(zeros, 0.0).then_inc(sem("zeroed"), 1)
            nc.vector.memset(keys[HD:P, 1, :].bitcast(F32), 0.0).then_inc(sem("dve_fill"), 1)
            nc.vector.memset(q_shift[HD:P, :, :, :].bitcast(F32), 0.0).then_inc(sem("q_fill"), 1)
            dve.wait_ge(sem("dve_fill"), 1)
            nc.vector.memset(keys[HD:HD + 2, 1, :].bitcast(F32), 1.0).then_inc(sem("keys_fill"), 1)
            for p in range(PAIRS):
                for a in range(2):
                    dve.wait_ge(sem("folded"), 4 * p + 2 * a + 1)
                    nc.vector.tensor_copy(w_qk[:, :, p, a * HD:(a + 1) * HD],
                                          banks[a].rearrange("p (c n) -> p c n", c=DC)[:, :, 0:HD]) \
                        .then_inc(sem("fold_copied"), 1)
                    dve.wait_ge(sem("folded"), 4 * p + 2 * a + 2)
                    nc.vector.tensor_copy(w_vo[a * HD:(a + 1) * HD, p, :], banks[2 + a][a * HD:(a + 1) * HD, 0:D]) \
                        .then_inc(sem("fold_copied"), 1)
            for tag in ("f1", "f2"):
                dve_stats(dve, tag)
                if tag == "f1":
                    dve.wait_ge(sem("masks"), 3)
                dve_rows(dve, tag)
                dve_route(dve, tag)
                dve_scatter(dve, tag)
                dve_experts(dve, tag)
                dve_gather(dve, tag)
                if tag == "f1":
                    dve_stats(dve, "att")
                    dve_rows(dve, "att")
                    dve_latents(dve)
                    dve_attention(dve)

        @block.scalar
        def _(act):
            act_std(act, "f1")
            act_transposed(act, "f1", True)
            act_exp_top(act, "f1")
            act_experts(act, "f1")
            act_std(act, "att")
            act_transposed(act, "att", False)
            act_latents(act)
            act_attention(act)
            act_std(act, "f2")
            act_transposed(act, "f2", True)
            act_exp_top(act, "f2")
            act_experts(act, "f2")

        @block.tensor
        def _(pe):
            pe.wait_ge(sem("raw_loaded"), 64)
            for p in range(PAIRS):
                for a in range(2):
                    h = slice(a * HD, (a + 1) * HD)
                    if p:
                        pe.wait_ge(sem("fold_copied"), 4 * (p - 1) + 2 * a + 2)
                    for c in range(DC):
                        last = nc.tensor.matmul(banks[a][:, 256 * c:256 * c + HD], q_raw[h, p, c * P:(c + 1) * P],
                                                k_raw[h, p, :], start=True, stop=True)
                    last.then_inc(sem("folded"), 1)
                    nc.tensor.matmul(banks[2 + a][h, 0:D], v_raw[h, p, :], o_raw[h, p, :],
                                     start=True, stop=True).then_inc(sem("folded"), 1)
            pe.wait_ge(sem("consts_loaded"), 48)
            pe.wait_ge(sem("masks"), 3)
            pe.wait_ge(sem("fold_copied"), 4 * PAIRS)
            pe_transposed(pe, "f1", True)
            pe_ranks(pe, "f1")
            pe_experts(pe, "f1")
            pe_transposed(pe, "att", False)
            pe_latents(pe)
            pe_attention(pe)
            pe_transposed(pe, "f2", True)
            pe_ranks(pe, "f2")
            pe_experts(pe, "f2")


_OUT = ((BATCH, SEQ, D), "float32")


def kernel(L0_attn_x, L0_attn_Wq, L0_attn_Wkv_down, L0_attn_Wk_up, L0_attn_Wv_up, L0_attn_Wo,
           L0_ffn_gate_w, L0_ffn_w_gate, L0_ffn_w_up, L0_ffn_w_down):
    import numpy as np
    import concourse.bacc as bacc
    from concourse.bass_utils import run_bass_kernel_spmd

    def rows(w):
        w = np.asarray(w)
        return w.reshape(-1, P, w.shape[-1]).transpose(1, 0, 2)

    gu = np.concatenate([np.asarray(L0_ffn_w_gate), np.asarray(L0_ffn_w_up)], axis=1)
    arrays = {
        "x_in": np.asarray(L0_attn_x),
        "gate_t": rows(np.asarray(L0_ffn_gate_w).T),
        "w_gu": gu.reshape(EXPERTS, 2 * INNER, DC, P).transpose(3, 0, 2, 1),
        "w_dn": np.asarray(L0_ffn_w_down).transpose(2, 0, 1),
        "w_q": rows(L0_attn_Wq),
        "w_k": rows(L0_attn_Wk_up),
        "w_v": rows(L0_attn_Wv_up),
        "w_o_t": rows(np.asarray(L0_attn_Wo).T),
        "w_kvd": rows(np.asarray(L0_attn_Wkv_down).T),
    }
    arrays = {name: np.ascontiguousarray(a) for name, a in arrays.items()}
    nc = bacc.Bacc("TRN2", target_bir_lowering=False, num_devices=1)
    args = [nc.dram_tensor(name, a.shape, F32, kind="ExternalInput").ap() for name, a in arrays.items()]
    out = nc.dram_tensor("out", _OUT[0], F32, kind="ExternalOutput").ap()
    build(nc, *args, out)
    r = run_bass_kernel_spmd(nc, [arrays], core_ids=[0])
    return r.results[0]["out"]
```

```python
from contextlib import ExitStack

import concourse.bass as bass
from concourse import mybir
from concourse.alu_op_type import AluOpType as ALU

ACT = mybir.ActivationFunctionType
F32 = mybir.dt.float32
F32R = mybir.dt.float32r
I32 = mybir.dt.int32
AX_X = mybir.AxisListType.X
ds = bass.ds

P = 128
D = 256
DC = D // P
BATCH = 4
SEQ = 1024
TOK = BATCH * SEQ
NT = TOK // P
HEADS = 8
HD = 64
PAIRS = HEADS // 2
EXPERTS = 8
INNER = 128
SLOT_TILES = NT + EXPERTS
SLOTS = SLOT_TILES * P
EPS = 1e-5
SCALE = HD ** -0.5
HALF = 512
QT = SEQ // P
KT = SEQ // P
STEPS = 2 * KT
MAXES = 2 * QT * 2
LOADS = 4
RING = 4
A_STEPS = (5, 7)


def build(nc, x_in, gate_t, w_gu, w_dn, w_q, w_k, w_v, w_o_t, w_kvd, out):
    with ExitStack() as ctx:
        def sb(name, shape, dt=F32):
            return ctx.enter_context(nc.sbuf_tensor(name, shape, dt))

        sems = {}

        def sem(name):
            if name not in sems:
                sems[name] = ctx.enter_context(nc.semaphore(name))
            return sems[name]

        sorted_x = nc.dram_tensor("sorted_x", [SLOTS, D], F32, kind="Internal").ap()
        sorted_y = nc.dram_tensor("sorted_y", [SLOTS, D], F32, kind="Internal").ap()

        x_res = sb("x_res", [P, NT * D])
        arena_a = sb("arena_a", [P, DC * TOK])
        arena_b = sb("arena_b", [P, 8192])
        keys = sb("keys", [P, 2, TOK], F32R)
        keys_now = sb("keys_now", [P, 2, SEQ], F32R)
        latent = sb("latent", [P, NT, HD])
        latent_now = sb("latent_now", [P, KT, HD])
        q_split = sb("q_split", [P, PAIRS, 2, SEQ], F32R)
        q_shift = sb("q_shift", [P, 2, 2, SEQ], F32R)
        w_qk = sb("w_qk", [P, DC, PAIRS, P])
        w_vo = sb("w_vo", [P, PAIRS, D])
        ident = sb("ident", [P, P])
        before = sb("before", [P, P])
        ones = sb("ones", [P, P])
        gate_w = sb("gate_w", [P, DC, EXPERTS])
        kvd = sb("kvd", [P, DC, P])
        stats = sb("stats", [P, NT, 6])
        st = sb("st", [P, 8, NT])
        slots = sb("slots", [P, NT], I32)
        slot_now = sb("slot_now", [P, RING], I32)
        tile_expert = sb("tile_expert", [P, SLOT_TILES], I32)
        small = sb("small", [P, 8, EXPERTS])
        small_i = sb("small_i", [P, EXPERTS], I32)
        eps_col = sb("eps_col", [P, 1])
        maxes = sb("maxes", [P, MAXES])
        top_q = sb("top_q", [P, 2 * QT])
        shift_q = sb("shift_q", [P, 4 * QT])
        shift_t = sb("shift_t", [4 * QT, P], F32R)
        denom = sb("denom", [P, 2, 4])
        inv_denom = sb("inv_denom", [P, 2, 4])

        xn_t = arena_a[:, :].rearrange("p (c n) -> p c n", c=DC)
        gu_sb = arena_a[:, 0:4096].rearrange("p (e c n) -> p e c n", e=EXPERTS, c=DC)
        dn_sb = arena_a[:, 4096:6144].rearrange("p (e n) -> p e n", e=EXPERTS)

        def route_tmp(n):
            return arena_a[:, 6144 + n * 256:6144 + (n + 1) * 256].rearrange("p (t e) -> p t e", e=EXPERTS)

        att_o = arena_b[:, 0:4096].rearrange("p (h n) -> p h n", h=PAIRS)
        prob = arena_b[:, 4096:6144].rearrange("p (b a n) -> p b a n", b=2, a=2)
        prob_sum = arena_b[:, 6144:8192].rearrange("p (b a n) -> p b a n", b=2, a=2)
        take_at = [0]

        def take(n, w):
            a = take_at[0]
            take_at[0] += n * w
            return arena_b[:, a:a + n * w].rearrange("p (b n) -> p b n", b=n)

        q_raw, k_raw, v_raw, o_raw = take(PAIRS, D), take(PAIRS, HD), take(PAIRS, HD), take(PAIRS, D)
        x_col = take(2, 2 * D)
        rows_out = take(RING, D)
        rows_in = take(RING, D)
        x_row = rows_in[:, :, :].rearrange("p (b j) n -> p b (j n)", b=2)
        rows_t = take(2, D)
        silu_g = take(2, INNER)
        hid = take(2, INNER)
        hid_t = take(2, INNER)
        y_rows = take(RING, D)
        zeros = y_rows[:, 0, :]
        lat_f = arena_b[:, 4096:4096 + 2 * HALF].rearrange("p (b n) -> p b n", b=2)
        assert take_at[0] <= 8192

        ps = [ctx.enter_context(nc.psum_tensor(f"ps{i}", [P, 2, HALF], F32)) for i in range(3)]
        ps_o = ctx.enter_context(nc.psum_tensor("ps_o", [P, HALF], F32))
        ps_x = ctx.enter_context(nc.psum_tensor("ps_x", [P, HALF], F32))
        banks = [ps[i][:, j, :] for i in range(3) for j in range(2)] + [ps_o[:, :], ps_x[:, :]]
        ps_s = ps[0:2]
        ps_m = [ps[2][:, j, :] for j in range(2)]

        x_tiles = x_in.rearrange("b (t p) d -> p (b t) d", p=P)
        out_tiles = out.rearrange("b (t p) d -> p (b t) d", p=P)

        def x_tile(t):
            return x_res[:, ds(t * D, D)] if not isinstance(t, int) else x_res[:, t * D:(t + 1) * D]

        def each(eng, n, body):
            body(0, True)
            with eng.Fori(1, n) as i:
                body(i, False)

        block = ctx.enter_context(nc.Block())


        def pe_transposed(pe, tag, logits):
            def logit(i, k):
                n = 2 * i + k
                pe.wait_ge(sem(f"col_ready_{tag}"), n + 1)
                for j in range(2):
                    for c in range(DC):
                        last = nc.tensor.matmul(banks[2][:, ds((2 * n + j) * EXPERTS, EXPERTS)],
                                                x_col[:, k, j * D + c * P:j * D + (c + 1) * P], gate_w[:, c, :],
                                                start=(c == 0), stop=(c == DC - 1))
                last.then_inc(sem(f"logit_{tag}"), 1)

            def body(i, first):
                for k in range(2):
                    n = 2 * i + k
                    pe.wait_ge(sem(f"row_ready_{tag}"), 2 * n + 2)
                    if not first:
                        pe.wait_ge(sem(f"col_ready_{tag}"), n - 1)
                    for j in range(2):
                        for c in range(DC):
                            last = nc.tensor.transpose(banks[k][:, j * D + c * P:j * D + (c + 1) * P],
                                                       x_row[:, k, j * D + c * P:j * D + (c + 1) * P], ident[:, :])
                    last.then_inc(sem(f"row_turned_{tag}"), 1)
                    if logits and k == 1:
                        logit(i, 0)
                    elif logits and not first:
                        logit(i - 1, 1)
            each(pe, NT // 4, body)
            if logits:
                logit(NT // 4 - 1, 1)

        def act_transposed(act, tag, logits):
            def body(i, first):
                for k in range(2):
                    n = 2 * i + k
                    act.wait_ge(sem(f"row_turned_{tag}"), n + 1)
                    if logits:
                        if not first:
                            act.wait_ge(sem(f"logit_{tag}"), n - 1)
                        nc.scalar.activation(x_col[:, k, :], banks[k], ACT.Copy) \
                            .then_inc(sem(f"col_ready_{tag}"), 1)
                    else:
                        nc.scalar.activation(
                            xn_t[:, :, ds(n * 2 * P, 2 * P)].rearrange("p c (j n) -> p c j n", j=2),
                            banks[k].rearrange("p (j c n) -> p c j n", j=2, c=DC), ACT.Copy) \
                            .then_inc(sem(f"col_ready_{tag}"), 1)
            each(act, NT // 4, body)

        def dve_rows(dve, tag):
            def body(i, first):
                for k in range(2):
                    for j in range(2):
                        t = 4 * i + 2 * k + j
                        if not first and j == 0:
                            dve.wait_ge(sem(f"row_turned_{tag}"), 2 * i + k - 1)
                        nc.vector.tensor_scalar(x_row[:, k, j * D:(j + 1) * D], x_tile(t), st[:, 4, ds(t, 1)],
                                                st[:, 5, ds(t, 1)], ALU.mult, ALU.add) \
                            .then_inc(sem(f"row_ready_{tag}"), 1)
            each(dve, NT // 4, body)

        link_count = [0]

        def link(ins):
            link_count[0] += 1
            ins.then_inc(sem("dve_link"), 1)
            nc.vector.wait_ge(sem("dve_link"), link_count[0])

        def tile_stats(t, tag):
            nc.vector.bn_stats(stats[:, ds(t, 1), :], x_tile(t)).then_inc(sem(f"stats_{tag}"), 1)

        def dve_stats(dve, tag):
            if tag == "f1":
                for g in range(LOADS):
                    dve.wait_ge(sem(f"x_loaded{g}"), 16)
                    with dve.Fori(g * NT // LOADS, (g + 1) * NT // LOADS) as t:
                        tile_stats(t, tag)
            dve.wait_ge(sem(f"stats_{tag}"), NT)
            nc.vector.tensor_tensor(st[:, 0, :], stats[:, :, 1], stats[:, :, 4], ALU.add)
            link(nc.vector.tensor_tensor(st[:, 1, :], stats[:, :, 1], stats[:, :, 4], ALU.subtract))
            nc.vector.tensor_tensor(st[:, 2, :], stats[:, :, 2], stats[:, :, 5], ALU.add)
            link(nc.vector.tensor_tensor(st[:, 1, :], st[:, 1, :], st[:, 1, :], ALU.mult))
            link(nc.vector.tensor_scalar(st[:, 2, :], st[:, 2, :], 1.0 / D, EPS, ALU.mult, ALU.add))
            link(nc.vector.scalar_tensor_tensor(st[:, 2, :], st[:, 1, :], 0.25, st[:, 2, :], ALU.mult, ALU.add))
            nc.vector.tensor_copy(st[:, 1, :], st[:, 2, :]).then_inc(sem(f"var_{tag}"), 1)
            dve.wait_ge(sem(f"std_{tag}"), 1)
            link(nc.vector.reciprocal(st[:, 4, :], st[:, 3, :]))
            link(nc.vector.tensor_tensor(st[:, 1, :], st[:, 4, :], st[:, 4, :], ALU.mult))
            link(nc.vector.tensor_tensor(st[:, 1, :], st[:, 1, :], st[:, 2, :], ALU.mult))
            link(nc.vector.tensor_scalar(st[:, 1, :], st[:, 1, :], -0.5, 1.5, ALU.mult, ALU.add))
            link(nc.vector.tensor_tensor(st[:, 4, :], st[:, 4, :], st[:, 1, :], ALU.mult))
            link(nc.vector.scalar_tensor_tensor(st[:, 5, :], st[:, 0, :], -0.5, st[:, 4, :], ALU.mult, ALU.mult))

        def act_std(act, tag):
            act.wait_ge(sem(f"var_{tag}"), 1)
            nc.scalar.activation(st[:, 3, :], st[:, 1, :], ACT.Sqrt).then_inc(sem(f"std_{tag}"), 1)


        def dve_route(dve, tag):
            top, rank, one_hot = st[:, 6, :], route_tmp(1), route_tmp(2)
            wide = [P, NT, EXPERTS]
            dve.wait_ge(sem(f"logit_{tag}"), NT // 2)
            lg = banks[2][:, 0:NT * EXPERTS].rearrange("p (t e) -> p t e", e=EXPERTS)
            link(nc.vector.tensor_reduce(top, lg, AX_X, ALU.max))
            nc.vector.tensor_copy(st[:, 7, :], top).then_inc(sem(f"top_{tag}"), 1)
            link(nc.vector.tensor_tensor(rank, lg, top.unsqueeze(2).to_broadcast(wide), ALU.is_equal))
            link(nc.vector.tensor_tensor(rank, rank, small[:, 7, :].unsqueeze(1).to_broadcast(wide), ALU.mult))
            link(nc.vector.tensor_reduce(top, rank, AX_X, ALU.max))
            link(nc.vector.tensor_tensor(one_hot, rank, top.unsqueeze(2).to_broadcast(wide), ALU.is_equal))
            nc.vector.tensor_copy(route_tmp(0), one_hot).then_inc(sem(f"one_hot_{tag}"), 1)
            dve.wait_ge(sem(f"exp_top_{tag}"), 1)
            link(nc.vector.tensor_scalar(st[:, 3, :], st[:, 3, :], 1.0, None, ALU.add))
            link(nc.vector.reciprocal(st[:, 3, :], st[:, 3, :]))
            nc.vector.tensor_tensor(st[:, 4, :], st[:, 4, :], st[:, 3, :], ALU.mult)
            link(nc.vector.tensor_tensor(st[:, 5, :], st[:, 5, :], st[:, 3, :], ALU.mult))
            dve.wait_ge(sem(f"ranks_{tag}"), 2)
            a, b = route_tmp(0), route_tmp(3)
            counts = banks[4][:, 0:NT * EXPERTS].rearrange("p (t e) -> p t e", e=EXPERTS)
            link(nc.vector.tensor_copy(a, counts))
            s = 1
            while s < NT:
                nc.vector.tensor_copy(b[:, 0:s, :], a[:, 0:s, :])
                link(nc.vector.tensor_tensor(b[:, s:NT, :], a[:, s:NT, :], a[:, 0:NT - s, :], ALU.add))
                a, b = b, a
                s *= 2
            n, up, end, base, tmp = (small[:, j, :] for j in range(5))
            link(nc.vector.tensor_scalar(n, a[:, NT - 1, :], float(P - 1), None, ALU.add))
            link(nc.vector.tensor_copy(small_i[:, :], n))
            link(nc.vector.tensor_scalar(small_i[:, :], small_i[:, :], 7, 7, ALU.logical_shift_right,
                                         ALU.logical_shift_left))
            link(nc.vector.tensor_copy(up, small_i[:, :]))
            link(nc.vector.tensor_copy(end, up))
            s, u, v = 1, end, tmp
            while s < EXPERTS:
                nc.vector.tensor_copy(v[:, 0:s], u[:, 0:s])
                link(nc.vector.tensor_tensor(v[:, s:EXPERTS], u[:, s:EXPERTS], u[:, 0:EXPERTS - s], ALU.add))
                u, v = v, u
                s *= 2
            link(nc.vector.tensor_tensor(base, u, up, ALU.subtract))
            within = banks[3][:, 0:NT * EXPERTS].rearrange("p (t e) -> p t e", e=EXPERTS)
            link(nc.vector.tensor_tensor(a, a, counts, ALU.subtract))
            link(nc.vector.tensor_tensor(a, a, within, ALU.add))
            link(nc.vector.tensor_tensor(a, a, base.unsqueeze(1).to_broadcast(wide), ALU.add))
            link(nc.vector.tensor_tensor(a, a, one_hot, ALU.mult))
            link(nc.vector.tensor_reduce(top, a, AX_X, ALU.add))
            nc.vector.tensor_copy(slots[:, :], top)
            tiles = [P, SLOT_TILES, EXPERTS]
            cmp_a = arena_a[:, 6144 + 1024:6144 + 1024 + SLOT_TILES * EXPERTS].rearrange("p (t e) -> p t e", e=EXPERTS)
            row0 = arena_a[:, 6144 + 1400:6144 + 1400 + SLOT_TILES]
            cnt = arena_a[:, 6144 + 1450:6144 + 1450 + SLOT_TILES]
            dve.wait_ge(sem(f"row0_{tag}"), 1)
            link(nc.vector.tensor_tensor(cmp_a, u.unsqueeze(1).to_broadcast(tiles),
                                         row0.unsqueeze(2).to_broadcast(tiles), ALU.is_le))
            link(nc.vector.tensor_reduce(cnt, cmp_a, AX_X, ALU.add))
            link(nc.vector.tensor_scalar(cnt, cnt, float(EXPERTS - 1), None, ALU.min))
            nc.vector.tensor_copy(tile_expert[:, :], cnt).then_inc(sem(f"tile_expert_{tag}"), 1)
            dve.wait_ge(sem(f"tile_expert_{tag}"), 1)

        def pool_row0(pool, tag):
            row0 = arena_a[:, 6144 + 1400:6144 + 1400 + SLOT_TILES]
            pool.iota(row0, [[P, SLOT_TILES]], base=0, channel_multiplier=0,
                      allow_small_or_imprecise_dtypes=True).then_inc(sem(f"row0_{tag}"), 1)

        def pe_ranks(pe, tag):
            pe.wait_ge(sem(f"one_hot_{tag}"), 1)
            hot = route_tmp(0).rearrange("p t e -> p (t e)")
            nc.tensor.matmul(banks[3][:, 0:NT * EXPERTS], before[:, :], hot, start=True, stop=True) \
                .then_inc(sem(f"ranks_{tag}"), 1)
            nc.tensor.matmul(banks[4][:, 0:NT * EXPERTS], ones[:, :], hot, start=True, stop=True) \
                .then_inc(sem(f"ranks_{tag}"), 1)

        def act_exp_top(act, tag):
            act.wait_ge(sem(f"top_{tag}"), 1)
            nc.scalar.activation(st[:, 3, :], st[:, 7, :], ACT.Exp, scale=-1.0).then_inc(sem(f"exp_top_{tag}"), 1)

        def dve_scatter(dve, tag):
            def body(i, first):
                for k in range(RING):
                    t = RING * i + k
                    if not first:
                        dve.wait_ge(sem(f"scattered{k}_{tag}"), 16 * i)
                    nc.vector.tensor_copy(slot_now[:, k:k + 1], slots[:, ds(t, 1)]) \
                        .then_inc(sem(f"to_scatter_{tag}"), 1)
                    nc.vector.tensor_scalar(rows_out[:, k, :], x_tile(t), st[:, 4, ds(t, 1)], st[:, 5, ds(t, 1)],
                                            ALU.mult, ALU.add).then_inc(sem(f"to_scatter_{tag}"), 1)
            each(dve, NT // RING, body)

        def pool_scatter(pool, tag):
            pool.wait_ge(sem("zero_filled"), 16)
            for t in range(NT):
                k = t % RING
                pool.wait_ge(sem(f"to_scatter_{tag}"), 2 * (t + 1))
                pool.indirect_dma_start(sorted_x[:, :], bass.IndirectOffsetOnAxis(ap=slot_now[:, k:k + 1], axis=0),
                                        rows_out[:, k, :], None).then_inc(sem(f"scattered{k}_{tag}"), 16)

        def sp_experts(sp, tag):
            for k in range(RING):
                sp.wait_ge(sem(f"scattered{k}_{tag}"), 16 * (NT // RING))

            def load(i, first):
                for k in range(RING):
                    t = RING * i + k
                    row = t * P if first else sp.snap(t * P)
                    if not first:
                        sp.wait_ge(sem(f"in_turned_{tag}"), t - RING + 1)
                    sp.dma_start(rows_in[:, k, :], sorted_x[ds(row, P), :]).then_inc(sem(f"in{k}_{tag}"), 16)

            load(0, True)
            with sp.Fori(1, SLOT_TILES // RING) as i:
                load(i, False)

        def old(t, n):
            return not isinstance(t, int) or t >= n

        def in_range(t):
            return not isinstance(t, int) or 0 <= t < SLOT_TILES

        def expert_tiles(eng, tile):
            groups = SLOT_TILES // RING
            for t in range(2 * RING):
                tile(t, t % RING)
            with eng.Fori(2, groups - 1) as i:
                for k in range(RING):
                    tile(RING * i + k, k)
            for t in range(SLOT_TILES - RING, SLOT_TILES + 3):
                tile(t, t % RING)

        def pe_experts(pe, tag):
            def turn(t, k):
                pe.wait_ge(sem(f"in{k}_{tag}"), 16 * (t // RING + 1) if isinstance(t, int) else (t - k) * 4 + 16)
                if old(t, 2):
                    pe.wait_ge(sem(f"in_copied_{tag}"), t - 1)
                for c in range(DC):
                    last = nc.tensor.transpose(banks[k % 2][:, c * P:(c + 1) * P], rows_in[:, k, c * P:(c + 1) * P],
                                               ident[:, :])
                last.then_inc(sem(f"in_turned_{tag}"), 1)

            def expert(t):
                return pe.value_load(tile_expert[0:1, ds(t, 1)], min_val=0, max_val=EXPERTS - 1)

            def gate_up(t, k):
                e = expert(t)
                pe.wait_ge(sem(f"in_copied_{tag}"), t + 1)
                if old(t, 2):
                    pe.wait_ge(sem(f"hid_{tag}"), t - 1)
                for c in range(DC):
                    last = nc.tensor.matmul(banks[2 + k % 2][:, 0:2 * INNER], rows_t[:, k % 2, c * P:(c + 1) * P],
                                            arena_a[:, ds(e * (DC * 2 * INNER) + c * 2 * INNER, 2 * INNER)],
                                            start=(c == 0), stop=(c == DC - 1))
                last.then_inc(sem(f"gate_up_{tag}"), 1)

            def turn_hidden(t, k):
                pe.wait_ge(sem(f"hid_{tag}"), t + 1)
                if old(t, 2):
                    pe.wait_ge(sem(f"hid_copied_{tag}"), t - 1)
                nc.tensor.transpose(banks[4 + k % 2][:, 0:P], hid[:, k % 2, :], ident[:, :]) \
                    .then_inc(sem(f"hid_turned_{tag}"), 1)

            def down(t, k):
                e = expert(t)
                pe.wait_ge(sem(f"hid_copied_{tag}"), t + 1)
                if old(t, 2):
                    pe.wait_ge(sem(f"y_ready_{tag}"), t - 1)
                nc.tensor.matmul(banks[6 + k % 2][:, 0:D], hid_t[:, k % 2, :], arena_a[:, ds(e * D + 4096, D)],
                                 start=True, stop=True).then_inc(sem(f"down_{tag}"), 1)

            def tile(t, k):
                if in_range(t):
                    gate_up(t, k)
                if in_range(t - 2):
                    down(t - 2, (k - 2) % RING)
                if in_range(t + 2):
                    turn(t + 2, (k + 2) % RING)
                if in_range(t - 1):
                    turn_hidden(t - 1, (k - 1) % RING)
            pe.wait_ge(sem(f"experts_loaded_{tag}"), 32)
            pe.wait_ge(sem(f"tile_expert_{tag}"), 1)
            turn(0, 0)
            turn(1, 1)
            expert_tiles(pe, tile)

        def act_experts(act, tag):
            def copy_in(t, k):
                act.wait_ge(sem(f"in_turned_{tag}"), t + 1)
                if old(t, 2):
                    act.wait_ge(sem(f"gate_up_{tag}"), t - 1)
                nc.scalar.activation(rows_t[:, k % 2, :], banks[k % 2][:, 0:D], ACT.Copy) \
                    .then_inc(sem(f"in_copied_{tag}"), 1)

            def silu(t, k):
                act.wait_ge(sem(f"gate_up_{tag}"), t + 1)
                if old(t, 2):
                    act.wait_ge(sem(f"hid_{tag}"), t - 1)
                nc.scalar.activation(silu_g[:, k % 2, :], banks[2 + k % 2][:, 0:INNER], ACT.Silu) \
                    .then_inc(sem(f"silu_{tag}"), 1)

            def store(t, k):
                row = t * P if isinstance(t, int) else act.snap(t * P)
                act.wait_ge(sem(f"y_ready_{tag}"), t + 1)
                act.dma_start(sorted_y[ds(row, P), :], y_rows[:, k, :]).then_inc(sem(f"y_stored{k}_{tag}"), 16)

            def tile(t, k):
                if in_range(t):
                    silu(t, k)
                if in_range(t + 2):
                    copy_in(t + 2, (k + 2) % RING)
                if in_range(t - 3):
                    store(t - 3, (k - 3) % RING)
            copy_in(0, 0)
            copy_in(1, 1)
            expert_tiles(act, tile)

        def dve_experts(dve, tag):
            def copy_hidden(t, k):
                dve.wait_ge(sem(f"hid_turned_{tag}"), t + 1)
                if old(t, 2):
                    dve.wait_ge(sem(f"down_{tag}"), t - 1)
                nc.vector.tensor_copy(hid_t[:, k % 2, :], banks[4 + k % 2][:, 0:P]) \
                    .then_inc(sem(f"hid_copied_{tag}"), 1)

            def gated(t, k):
                dve.wait_ge(sem(f"silu_{tag}"), t + 1)
                if old(t, 2):
                    dve.wait_ge(sem(f"hid_turned_{tag}"), t - 1)
                nc.vector.tensor_tensor(hid[:, k % 2, :], silu_g[:, k % 2, :], banks[2 + k % 2][:, INNER:2 * INNER],
                                        ALU.mult).then_inc(sem(f"hid_{tag}"), 1)

            def y_out(t, k):
                dve.wait_ge(sem(f"down_{tag}"), t + 1)
                if old(t, RING):
                    dve.wait_ge(sem(f"y_stored{k}_{tag}"), 16 * (t // RING) if isinstance(t, int) else (t - k) * 4)
                nc.vector.tensor_copy(y_rows[:, k, :], banks[6 + k % 2][:, 0:D]).then_inc(sem(f"y_ready_{tag}"), 1)

            def tile(t, k):
                if in_range(t - 2):
                    copy_hidden(t - 2, (k - 2) % RING)
                if in_range(t):
                    gated(t, k)
                if in_range(t - 2):
                    y_out(t - 2, (k - 2) % RING)
            expert_tiles(dve, tile)

        def pool_gather(pool, tag):
            for k in range(RING):
                pool.wait_ge(sem(f"y_stored{k}_{tag}"), 16 * (SLOT_TILES // RING))
            for t in range(NT):
                k = t % RING
                pool.wait_ge(sem(f"slot_back_{tag}"), t + 1)
                pool.indirect_dma_start(rows_out[:, k, :], None, sorted_y[:, :],
                                        bass.IndirectOffsetOnAxis(ap=slot_now[:, k:k + 1], axis=0)) \
                    .then_inc(sem(f"gathered{k}_{tag}"), 16)

        def dve_gather(dve, tag):
            for k in range(RING):
                dve.wait_ge(sem(f"scattered{k}_{tag}"), 16 * (NT // RING))
                nc.vector.tensor_copy(slot_now[:, k:k + 1], slots[:, k:k + 1]).then_inc(sem(f"slot_back_{tag}"), 1)

            def body(i, last):
                for k in range(RING):
                    t = RING * i + k
                    dve.wait_ge(sem(f"gathered{k}_{tag}"), 16 * i + 16)
                    nc.vector.scalar_tensor_tensor(x_tile(t), rows_out[:, k, :], 0.5, x_tile(t),
                                                   ALU.mult, ALU.add).then_inc(sem(f"ffn_added_{tag}"), 1)
                    if not last or tag == "f1":
                        dve.wait_ge(sem(f"ffn_added_{tag}"), t + 1)
                    if tag == "f1":
                        tile_stats(t, "att")
                    if not last:
                        nc.vector.tensor_copy(slot_now[:, k:k + 1], slots[:, ds(t + RING, 1)]) \
                            .then_inc(sem(f"slot_back_{tag}"), 1)
            with dve.Fori(0, NT // RING - 1) as i:
                body(i, False)
            body(NT // RING - 1, True)
            dve.wait_ge(sem(f"ffn_added_{tag}"), NT)


        def pe_queries(pe, slot, c, tokens, use):
            for d in range(DC):
                last = nc.tensor.matmul(ps_x[:, :], w_qk[:, d, slot, :], xn_t[:, d, ds(tokens, HALF)],
                                        start=(d == 0), stop=(d == DC - 1))
            last.then_inc(sem("q_made"), 1)

        def act_queries(act, slot, c, n):
            act.wait_ge(sem("q_made"), n + 1)
            for a in range(2):
                nc.scalar.activation(q_split[0:HD, slot, a, c * HALF:(c + 1) * HALF], ps_x[a * HD:(a + 1) * HD, :],
                                     ACT.Copy).then_inc(sem("q_hi"), 1)

        def dve_queries(dve, slot, c, n):
            for a in range(2):
                dve.wait_ge(sem("q_hi"), 2 * n + 2)
                nc.vector.tensor_tensor(q_split[HD:P, slot, a, c * HALF:(c + 1) * HALF], ps_x[a * HD:(a + 1) * HD, :],
                                        q_split[0:HD, slot, a, c * HALF:(c + 1) * HALF].bitcast(F32), ALU.subtract) \
                    .then_inc(sem("q_lo"), 1)

        def pe_max(pe, slot, m, key0, n, first):
            a, qt, half = m // (2 * QT), m // 2 % QT, m % 2
            if not first:
                pe.wait_ge(sem("max_taken"), n - 1)
            nc.tensor.matmul(ps_m[m % 2], q_split[:, slot, a, qt * P:(qt + 1) * P],
                             keys[:, 0, ds(key0 + half * HALF, HALF)], start=True, stop=True) \
                .then_inc(sem("max_scores"), 1)

        def dve_max(dve, m, n):
            dve.wait_ge(sem("max_scores"), n + 1)
            nc.vector.tensor_reduce(maxes[:, m:m + 1], ps_m[m % 2], AX_X, ALU.max).then_inc(sem("max_taken"), 1)

        def dve_shift(dve, n, u):
            dve.wait_ge(sem("max_taken"), n)
            pairs = maxes[:, :].rearrange("p (q h) -> p q h", h=2)
            hi = shift_q[:, :].rearrange("p (a s q) -> p a s q", a=2, s=2)
            nc.vector.tensor_tensor(top_q[:, :], pairs[:, :, 0], pairs[:, :, 1], ALU.max) \
                .then_inc(sem("shift_top"), 1)
            dve.wait_ge(sem("shift_top"), u + 1)
            top = top_q[:, :].rearrange("p (a q) -> p a q", a=2)
            if not isinstance(u, int) or u > 0:
                dve.wait_ge(sem("shift_turned"), u)
            nc.vector.tensor_scalar(hi[:, :, 0, :].bitcast(F32R), top, -1.0, None, ALU.mult) \
                .then_inc(sem("shift_hi"), 1)
            dve.wait_ge(sem("shift_hi"), u + 1)
            nc.vector.scalar_tensor_tensor(hi[:, :, 1, :].bitcast(F32R), top, -1.0, hi[:, :, 0, :],
                                           ALU.mult, ALU.subtract).then_inc(sem("shift_lo"), 1)

        def pe_shift(pe, u):
            pe.wait_ge(sem("shift_lo"), u + 1)
            nc.tensor.transpose(ps_x[0:4 * QT, 0:P], shift_q[:, :], ident[:, :]).then_inc(sem("shift_turned"), 1)

        def act_shift(act, u, b=None, p=None):
            act.wait_ge(sem("shift_turned"), u + 1)
            if b is not None:
                act.wait_ge(sem(f"shift_placed{p % 2}"), 32 * (2 * b + p // 2 + 1))
            nc.scalar.activation(shift_t[:, :], ps_x[0:4 * QT, 0:P], ACT.Copy).then_inc(sem("shift_copied"), 1)

        def sp_shift(sp, slot, u):
            sp.wait_ge(sem("shift_copied"), u + 1)
            for a in range(2):
                sp.dma_start(q_shift[HD:HD + 2, slot % 2, a, :].bitcast(F32),
                             shift_t[2 * QT * a:2 * QT * (a + 1), :].bitcast(F32)).then_inc(sem(f"shift_placed{slot % 2}"), 16)

        def sp_queries(sp, slot):
            sp.dma_start(q_shift[0:HD, slot % 2, :, :].bitcast(F32), q_split[0:HD, slot, :, :].bitcast(F32)).then_inc(sem(f"q_copied{slot % 2}"), 16)

        def pe_latents(pe):
            def make(j):
                if j >= 2:
                    pe.wait_ge(sem("lat_lo"), j - 1)
                for d in range(DC):
                    last = nc.tensor.matmul(banks[2 + j % 2], kvd[:, d, :], xn_t[:, d, j * HALF:(j + 1) * HALF],
                                            start=(d == 0), stop=(d == DC - 1))
                last.then_inc(sem("lat_made"), 1)
            pe.wait_ge(sem("col_ready_att"), NT // 2)
            make(0)
            for j in range(TOK // HALF):
                if j + 1 < TOK // HALF:
                    make(j + 1)
                pe.wait_ge(sem("lat_f"), j + 1)
                if j >= 2:
                    pe.wait_ge(sem("lat_rows"), j - 1)
                for g in range(4):
                    last = nc.tensor.transpose(banks[4 + j % 2][:, g * P:(g + 1) * P],
                                               lat_f[:, j % 2, g * P:(g + 1) * P], ident[:, :])
                last.then_inc(sem("lat_turned"), 1)

        def act_latents(act):
            for j in range(TOK // HALF):
                act.wait_ge(sem("lat_made"), j + 1)
                if j >= 2:
                    act.wait_ge(sem("lat_turned"), j - 1)
                nc.scalar.activation(lat_f[:, j % 2, :], banks[2 + j % 2], ACT.Copy).then_inc(sem("lat_f"), 1)
                nc.scalar.activation(keys[:, 0, j * HALF:(j + 1) * HALF], banks[2 + j % 2], ACT.Copy) \
                    .then_inc(sem("lat_hi"), 1)

        def dve_latents(dve):
            for j in range(TOK // HALF):
                cols = slice(j * HALF, (j + 1) * HALF)
                dve.wait_ge(sem("lat_hi"), j + 1)
                nc.vector.tensor_tensor(keys[0:HD, 1, cols], banks[2 + j % 2][0:HD, :],
                                        keys[0:HD, 0, cols].bitcast(F32), ALU.subtract).then_inc(sem("lat_lo"), 1)
                dve.wait_ge(sem("lat_turned"), j + 1)
                nc.vector.tensor_copy(latent[:, 4 * j:4 * j + 4, :],
                                      banks[4 + j % 2].rearrange("p (g n) -> p g n", g=4)[:, :, 0:HD]) \
                    .then_inc(sem("lat_rows"), 1)

        def max_at(s):
            return min(5 * s // 2, MAXES)

        STEP_B = PAIRS * STEPS
        SUM_B = PAIRS * 2 * (KT - 1)

        def pe_attention(pe):
            pe.wait_ge(sem("lat_rows"), TOK // HALF)
            pe.wait_ge(sem("lat_lo"), TOK // HALF)
            for n in range(4):
                if n:
                    pe.wait_ge(sem("q_lo"), 2 * n)
                pe_queries(pe, n // 2, n % 2, (n % 2) * HALF, n)
            pe.wait_ge(sem("q_lo"), 8)
            for m in range(MAXES):
                pe_max(pe, 0, m, 0, m, m < 2)
            pe_shift(pe, 0)
            pe.wait_ge(sem("batch_ready"), 48)
            pe.wait_ge(sem("keys_fill"), 1)
            pe.wait_ge(sem("q_fill"), 1)

            with pe.Fori(0, BATCH) as b:
                bn = (b + 1) % BATCH

                def scores(p, s, a):
                    c, kt = s // KT, s % KT
                    n = p * STEPS + s
                    if n == 0 and a == 0:
                        pe.wait_ge(sem("batch_ready"), 48 * b + 48)
                    if n >= 2 and a == 0:
                        pe.wait_ge(sem("exp_done"), STEP_B * b + n - 1)
                    if s == 0 and a == 0:
                        pe.wait_ge(sem(f"q_copied{p % 2}"), 16 * (2 * b + p // 2 + 1))
                        pe.wait_ge(sem(f"shift_placed{p % 2}"), 32 * (2 * b + p // 2 + 1))
                    o = ps_s[n % 2][:, a, :]
                    q = slice(c * HALF, (c + 1) * HALF)
                    k = slice(kt * P, (kt + 1) * P)
                    nc.tensor.matmul(o, keys_now[:, 0, k], q_split[:, p, a, q], start=True, stop=False)
                    last = nc.tensor.matmul(o, keys_now[:, 1, k], q_shift[:, p % 2, a, q], start=False, stop=True)
                    if a == 1:
                        last.then_inc(sem("scored"), 1)

                def values(p, s):
                    c, kt = s // KT, s % KT
                    n = p * STEPS + s
                    pe.wait_ge(sem("exp_done"), STEP_B * b + n + 1)
                    if kt == 0 and p + c:
                        pe.wait_ge(sem("o_copied"), 2 * PAIRS * b + 2 * p + c)
                    for a in range(2):
                        src = prob_sum[:, c, a, :] if kt == 0 else prob[:, kt % 2, a, :]
                        last = nc.tensor.matmul(ps_o[a * HD:(a + 1) * HD, :], latent_now[:, kt, :], src,
                                                start=(kt == 0), stop=(kt == KT - 1))
                    last.then_inc(sem("valued"), 1)

                def turn_sum(p, c, a):
                    if a == 0:
                        pe.wait_ge(sem("summed"), SUM_B * b + (2 * p + c + 1) * (KT - 1))
                    if p + c + a:
                        pe.wait_ge(sem("denom"), 4 * PAIRS * b + 4 * p + 2 * c + a)
                    for g in range(4):
                        last = nc.tensor.transpose(ps_x[:, g * P:(g + 1) * P],
                                                   prob_sum[:, c, a, g * P:(g + 1) * P], ident[:, :])
                    last.then_inc(sem("sum_turned"), 1)

                def spread(p, c):
                    pe.wait_ge(sem("inv_denom"), 2 * PAIRS * b + 2 * p + c + 1)
                    for g in range(4):
                        for a in range(2):
                            last = nc.tensor.matmul(ps_x[a * HD:(a + 1) * HD, g * P:(g + 1) * P],
                                                    inv_denom[:, a, g:g + 1].to_broadcast([P, HD]), ident[:, :],
                                                    start=True, stop=True)
                    last.then_inc(sem("spread"), 1)

                for p in range(PAIRS):
                    wrap_m, wrap_a = p == PAIRS - 1, p >= PAIRS - 2
                    for s in range(STEPS):
                        todo = list(range(max_at(s), max_at(s + 1)))

                        def piece():
                            if todo:
                                m = todo.pop(0)
                                if m == 0:
                                    pe.wait_ge(sem("q_lo"), 4 * PAIRS * b + 4 * (p + 1) + 4)
                                pe_max(pe, (p + 1) % PAIRS, m, (bn if wrap_m else b) * SEQ,
                                       MAXES * PAIRS * b + MAXES * (p + 1) + m, False)
                        scores(p, s, 0)
                        piece()
                        scores(p, s, 1)
                        piece()
                        if p or s:
                            values(p - (s == 0), (s - 1) % STEPS)
                        piece()
                        if p and s in (2, 3):
                            turn_sum(p - 1, 1, s - 2)
                        if p and s == 4:
                            spread(p - 1, 1)
                        if s in A_STEPS:
                            c = A_STEPS.index(s)
                            n = 2 * PAIRS * b + 2 * (p + 2) + c
                            pe.wait_ge(sem("q_lo"), 2 * n)
                            if p:
                                pe.wait_ge(sem("normed"), 2 * PAIRS * b + 2 * p)
                            pe_queries(pe, (p + 2) % PAIRS, c, (bn if wrap_a else b) * SEQ + c * HALF, n)
                        if s in (10, 11):
                            if s == 10:
                                pe.wait_ge(sem("q_lo"), 4 * PAIRS * b + 4 * (p + 3))
                            turn_sum(p, 0, s - 10)
                        if s == 12:
                            spread(p, 0)
                        if s == 14:
                            pe.wait_ge(sem("normed"), 2 * PAIRS * b + 2 * p + 1)
                            pe_shift(pe, PAIRS * b + p + 1)
                values(PAIRS - 1, STEPS - 1)
                def project(t):
                    if t >= 2:
                        pe.wait_ge(sem("att_added"), QT * b + t - 1)
                    else:
                        pe.wait_ge(sem("max_taken"), MAXES * PAIRS * b + MAXES * (PAIRS + 1))
                    for p in range(PAIRS):
                        last = nc.tensor.matmul(ps_m[t % 2][:, 0:D], att_o[:, p, t * P:(t + 1) * P], w_vo[:, p, :],
                                                start=(p == 0), stop=(p == PAIRS - 1))
                    last.then_inc(sem("projected"), 1)
                for t in range(QT // 2):
                    project(t)
                pe.wait_ge(sem("shift_copied"), PAIRS * b + PAIRS + 1)
                turn_sum(PAIRS - 1, 1, 0)
                turn_sum(PAIRS - 1, 1, 1)
                spread(PAIRS - 1, 1)
                pe.wait_ge(sem("normed"), 2 * PAIRS * b + 2 * PAIRS)
                for t in range(QT // 2, QT):
                    project(t)
                pe.wait_ge(sem("att_added"), QT * b + QT)

        def act_attention(act):
            for n in range(4):
                act_queries(act, n // 2, n % 2, n)
            act_shift(act, 0)
            with act.Fori(0, BATCH) as b:
                def exps(p, s):
                    c, kt = s // KT, s % KT
                    n = p * STEPS + s
                    act.wait_ge(sem("scored"), STEP_B * b + n + 1)
                    k = 2 * p + c
                    if kt == 0:
                        if p:
                            act.wait_ge(sem("sum_turned"), 4 * PAIRS * b + 4 * (p - 1) + 2 * c + 2)
                    else:
                        g = k * (KT - 1) + kt - 1
                        used_sum = g - (1 if kt == 1 else 3 if kt == 2 else 2)
                        used_val = n - (2 if kt >= 3 else 2 if kt == 1 else 4)
                        if used_sum >= 0:
                            act.wait_ge(sem("summed"), SUM_B * b + used_sum + 1)
                            act.wait_ge(sem("valued"), STEP_B * b + used_val + 1)
                    dst = prob_sum[:, c, :, :] if kt == 0 else prob[:, kt % 2, :, :]
                    nc.scalar.activation(dst, ps_s[n % 2][:, :, :], ACT.Exp, scale=SCALE).then_inc(sem("exp_done"), 1)

                def copy_o(p, c):
                    act.wait_ge(sem("valued"), STEP_B * b + p * STEPS + (c + 1) * KT)
                    nc.scalar.activation(att_o[:, p, c * HALF:(c + 1) * HALF], ps_o[:, :], ACT.Copy) \
                        .then_inc(sem("o_copied"), 1)

                for p in range(PAIRS):
                    for s in range(STEPS):
                        exps(p, s)
                        if s == 0 and p:
                            copy_o(p - 1, 1)
                        if s == KT:
                            copy_o(p, 0)
                        if s in A_STEPS:
                            c = A_STEPS.index(s)
                            act_queries(act, (p + 2) % PAIRS, c, 2 * PAIRS * b + 2 * (p + 2) + c)
                        if s == 14:
                            act_shift(act, PAIRS * b + p + 1, b, p)
                copy_o(PAIRS - 1, 1)

        def dve_attention(dve):
            for n in range(4):
                dve_queries(dve, n // 2, n % 2, n)
            for m in range(MAXES):
                dve_max(dve, m, m)
            dve_shift(dve, MAXES, 0)
            with dve.Fori(0, BATCH) as b:
                def denoms(p, c, a):
                    n = 4 * PAIRS * b + 4 * p + 2 * c + a
                    dve.wait_ge(sem("sum_turned"), n + 1)
                    if a == 0 and p + c:
                        dve.wait_ge(sem("inv_denom"), 2 * PAIRS * b + 2 * p + c)
                    nc.vector.tensor_reduce(denom[:, a, :], ps_x[:, :].rearrange("p (g n) -> p g n", g=4), AX_X,
                                            ALU.add).then_inc(sem("denom"), 1)
                    if a == 1:
                        dve.wait_ge(sem("denom"), n + 1)
                        if p + c:
                            dve.wait_ge(sem("spread"), 2 * PAIRS * b + 2 * p + c)
                        nc.vector.reciprocal(inv_denom[:, :, :], denom[:, :, :]).then_inc(sem("inv_denom"), 1)

                def norm(p, c):
                    dve.wait_ge(sem("spread"), 2 * PAIRS * b + 2 * p + c + 1)
                    dve.wait_ge(sem("o_copied"), 2 * PAIRS * b + 2 * p + c + 1)
                    o = att_o[:, p, c * HALF:(c + 1) * HALF]
                    nc.vector.tensor_tensor(o, o, ps_x[:, :], ALU.mult).then_inc(sem("normed"), 1)

                for p in range(PAIRS):
                    for s in range(STEPS):
                        for m in range(max_at(s), max_at(s + 1)):
                            dve_max(dve, m, MAXES * PAIRS * b + MAXES * (p + 1) + m)
                        if p and s in (2, 3):
                            denoms(p - 1, 1, s - 2)
                        if p and s == 4:
                            norm(p - 1, 1)
                        if s in A_STEPS:
                            c = A_STEPS.index(s)
                            dve_queries(dve, (p + 2) % PAIRS, c, 2 * PAIRS * b + 2 * (p + 2) + c)
                        if s in (10, 11):
                            denoms(p, 0, s - 10)
                        if s == 12:
                            norm(p, 0)
                        if s == 13:
                            dve_shift(dve, MAXES * PAIRS * b + MAXES * (p + 2), PAIRS * b + p + 1)

                def add_projected(t):
                    dve.wait_ge(sem("projected"), QT * b + t + 1)
                    x = x_res[:, ds((b * QT + t) * D, D)]
                    nc.vector.tensor_tensor(x, x, ps_m[t % 2][:, 0:D], ALU.add).then_inc(sem("att_added"), 1)
                    dve.wait_ge(sem("att_added"), QT * b + t + 1)
                    tile_stats(b * QT + t, "f2")
                for t in range(QT // 2):
                    add_projected(t)
                denoms(PAIRS - 1, 1, 0)
                denoms(PAIRS - 1, 1, 1)
                norm(PAIRS - 1, 1)
                for t in range(QT // 2, QT):
                    add_projected(t)
            dve.wait_ge(sem("att_added"), NT)

        def pool_attention(pool):
            with pool.Fori(0, BATCH) as b:
                for p in range(PAIRS):
                    for c in range(2):
                        for kt in range(1, KT):
                            n = p * STEPS + c * KT + kt
                            k = 2 * p + c
                            pool.wait_ge(sem("exp_done"), STEP_B * b + n + 1)
                            if kt == 1:
                                pool.wait_ge(sem("valued"), STEP_B * b + n)
                            else:
                                pool.wait_ge(sem("summed"), SUM_B * b + k * (KT - 1) + kt - 1)
                            t = prob_sum[:, c, :, :].rearrange("p a n -> p (a n)")
                            nc.gpsimd.tensor_tensor(t, t, prob[:, kt % 2, :, :].rearrange("p a n -> p (a n)"), ALU.add) \
                                .then_inc(sem("summed"), 1)

        def sp_attention(sp):
            def batch(b, ready):
                key0, tile0 = (0, 0) if isinstance(b, int) else (sp.snap(b * SEQ), sp.snap(b * KT))
                ready()
                sp.dma_start(keys_now[:, 0, :].bitcast(F32), keys[:, 0, ds(key0, SEQ)].bitcast(F32)).then_inc(sem("batch_ready"), 16)
                sp.dma_start(keys_now[:, 1, :].bitcast(F32), keys[:, 1, ds(key0, SEQ)].bitcast(F32)).then_inc(sem("batch_ready"), 16)
                sp.dma_start(latent_now[:, :, :], latent[:, ds(tile0, KT), :]).then_inc(sem("batch_ready"), 16)
            sp.wait_ge(sem("lat_rows"), TOK // HALF)
            sp.wait_ge(sem("lat_lo"), TOK // HALF)
            sp.wait_ge(sem("keys_fill"), 1)
            batch(0, lambda: None)
            sp.wait_ge(sem("q_hi"), 8)
            sp.wait_ge(sem("q_fill"), 1)
            sp_queries(sp, 0)
            sp_shift(sp, 0, 0)
            with sp.Fori(0, BATCH) as b:
                for p in range(PAIRS):
                    if p:
                        sp.wait_ge(sem("scored"), STEP_B * b + STEPS * p)
                    sp_queries(sp, (p + 1) % PAIRS)
                    sp_shift(sp, (p + 1) % PAIRS, PAIRS * b + p + 1)

                def used_up():
                    sp.wait_ge(sem("valued"), STEP_B * b + STEP_B)
                batch((b + 1) % BATCH, used_up)
            sp.wait_ge(sem("batch_ready"), 48 * (BATCH + 1))
            for k in range(2):
                n = BATCH * PAIRS // 2 + 1 - k
                sp.wait_ge(sem(f"q_copied{k}"), 16 * n)
                sp.wait_ge(sem(f"shift_placed{k}"), 32 * n)


        @block.sync
        def _(sp):
            for g in range(LOADS):
                n = NT // LOADS
                sp.dma_start(x_res[:, g * n * D:(g + 1) * n * D].rearrange("p (t d) -> p t d", d=D),
                             x_tiles[:, g * n:(g + 1) * n, :]).then_inc(sem(f"x_loaded{g}"), 16)
            sp.wait_ge(sem("zeroed"), 1)
            sp.dma_start(sorted_x.rearrange("(n p) d -> p n d", p=P),
                         zeros.unsqueeze(1).to_broadcast([P, SLOT_TILES, D])).then_inc(sem("zero_filled"), 16)
            sp.dma_start(gu_sb, w_gu).then_inc(sem("experts_loaded_f1"), 16)
            sp.dma_start(dn_sb, w_dn).then_inc(sem("experts_loaded_f1"), 16)
            sp_experts(sp, "f1")
            sp_attention(sp)
            sp.wait_ge(sem("att_added"), NT)
            sp.dma_start(gu_sb, w_gu).then_inc(sem("experts_loaded_f2"), 16)
            sp.dma_start(dn_sb, w_dn).then_inc(sem("experts_loaded_f2"), 16)
            sp_experts(sp, "f2")
            with sp.Fori(0, NT) as t:
                col = sp.snap(t * D)
                sp.wait_ge(sem("ffn_added_f2"), t + 1)
                sp.dma_start(out_tiles[:, ds(t, 1), :], x_res[:, ds(col, D)].unsqueeze(1)) \
                    .then_inc(sem("out_stored"), 16)
            sp.wait_ge(sem("out_stored"), 16 * NT)

        @block.gpsimd
        def _(pool):
            def mask(dst, compare, name, fill, base):
                pool.affine_select(out=base, in_=base, pattern=[[-1, P]], compare_op=compare, fill=fill,
                                   base=0, channel_multiplier=1).then_inc(sem(name), 1)
            pool.memset(zeros, 0.0).then_inc(sem("zeroed"), 1)
            pool.memset(ones[:, :], 1.0).then_inc(sem("filled"), 1)
            pool.memset(ident[:, :], 0.0).then_inc(sem("filled"), 1)
            pool.memset(before[:, :], 0.0).then_inc(sem("filled"), 1)
            pool.wait_ge(sem("filled"), 3)
            mask(ident, ALU.not_equal, "masks", 1.0, ident[:, :])
            mask(before, ALU.is_ge, "masks", 1.0, before[:, :])
            pool.iota(small[:, 7, :], [[-1, EXPERTS]], base=EXPERTS, channel_multiplier=0,
                      allow_small_or_imprecise_dtypes=True).then_inc(sem("masks"), 1)
            pool_row0(pool, "f1")
            pool_scatter(pool, "f1")
            pool_gather(pool, "f1")
            pool_attention(pool)
            pool.wait_ge(sem("att_added"), NT)
            pool_row0(pool, "f2")
            pool_scatter(pool, "f2")
            pool_gather(pool, "f2")

        @block.vector
        def _(dve):
            for tag in ("f1", "f2"):
                dve_stats(dve, tag)
                if tag == "f1":
                    dve.wait_ge(sem("masks"), 3)
                dve_rows(dve, tag)
                dve_route(dve, tag)
                dve_scatter(dve, tag)
                if tag == "f1":
                    nc.vector.memset(keys[HD:P, 1, :].bitcast(F32), 0.0).then_inc(sem("keys_zero"), 1)
                    nc.vector.memset(q_shift[HD:P, :, :, :].bitcast(F32), 0.0).then_inc(sem("q_fill"), 1)
                    dve.wait_ge(sem("keys_zero"), 1)
                    nc.vector.memset(keys[HD:HD + 2, 1, :].bitcast(F32), 1.0).then_inc(sem("keys_fill"), 1)
                dve_experts(dve, tag)
                dve_gather(dve, tag)
                if tag == "f1":
                    dve_stats(dve, "att")
                    dve_rows(dve, "att")
                    dve_latents(dve)
                    dve_attention(dve)

        @block.scalar
        def _(act):
            for dst, src in ((q_raw, w_q), (k_raw, w_k), (v_raw, w_v), (o_raw, w_o_t)):
                act.dma_start(dst, src).then_inc(sem("raw_loaded"), 16)
            act.dma_start(gate_w[:, :, :], gate_t).then_inc(sem("consts_loaded"), 16)
            for half in range(2):
                act.dma_start(kvd[:, :, half * HD:(half + 1) * HD], w_kvd).then_inc(sem("consts_loaded"), 16)
            for p in range(PAIRS):
                for a in range(2):
                    act.wait_ge(sem("folded"), 4 * p + 2 * a + 1)
                    nc.scalar.activation(w_qk[:, :, p, a * HD:(a + 1) * HD],
                                         banks[a].rearrange("p (c n) -> p c n", c=DC)[:, :, 0:HD], ACT.Copy) \
                        .then_inc(sem("fold_copied"), 1)
                    act.wait_ge(sem("folded"), 4 * p + 2 * a + 2)
                    nc.scalar.activation(w_vo[a * HD:(a + 1) * HD, p, :], banks[2 + a][a * HD:(a + 1) * HD, 0:D],
                                         ACT.Copy) \
                        .then_inc(sem("fold_copied"), 1)
            act_std(act, "f1")
            act_transposed(act, "f1", True)
            act_exp_top(act, "f1")
            act_experts(act, "f1")
            act_std(act, "att")
            act_transposed(act, "att", False)
            act_latents(act)
            act_attention(act)
            act_std(act, "f2")
            act_transposed(act, "f2", True)
            act_exp_top(act, "f2")
            act_experts(act, "f2")

        @block.tensor
        def _(pe):
            pe.wait_ge(sem("raw_loaded"), 64)
            for p in range(PAIRS):
                for a in range(2):
                    h = slice(a * HD, (a + 1) * HD)
                    if p:
                        pe.wait_ge(sem("fold_copied"), 4 * (p - 1) + 2 * a + 2)
                    for c in range(DC):
                        last = nc.tensor.matmul(banks[a][:, 256 * c:256 * c + HD], q_raw[h, p, c * P:(c + 1) * P],
                                                k_raw[h, p, :], start=True, stop=True)
                    last.then_inc(sem("folded"), 1)
                    nc.tensor.matmul(banks[2 + a][h, 0:D], v_raw[h, p, :], o_raw[h, p, :],
                                     start=True, stop=True).then_inc(sem("folded"), 1)
            pe.wait_ge(sem("consts_loaded"), 48)
            pe.wait_ge(sem("masks"), 3)
            pe.wait_ge(sem("fold_copied"), 4 * PAIRS)
            pe_transposed(pe, "f1", True)
            pe_ranks(pe, "f1")
            pe_experts(pe, "f1")
            pe_transposed(pe, "att", False)
            pe_latents(pe)
            pe_attention(pe)
            pe_transposed(pe, "f2", True)
            pe_ranks(pe, "f2")
            pe_experts(pe, "f2")


_OUT = ((BATCH, SEQ, D), "float32")


def kernel(L0_attn_x, L0_attn_Wq, L0_attn_Wkv_down, L0_attn_Wk_up, L0_attn_Wv_up, L0_attn_Wo,
           L0_ffn_gate_w, L0_ffn_w_gate, L0_ffn_w_up, L0_ffn_w_down):
    import numpy as np
    import concourse.bacc as bacc
    from concourse.bass_utils import run_bass_kernel_spmd

    def rows(w):
        w = np.asarray(w)
        return w.reshape(-1, P, w.shape[-1]).transpose(1, 0, 2)

    gu = np.concatenate([np.asarray(L0_ffn_w_gate), np.asarray(L0_ffn_w_up)], axis=1)
    arrays = {
        "x_in": np.asarray(L0_attn_x),
        "gate_t": rows(np.asarray(L0_ffn_gate_w).T),
        "w_gu": gu.reshape(EXPERTS, 2 * INNER, DC, P).transpose(3, 0, 2, 1),
        "w_dn": np.asarray(L0_ffn_w_down).transpose(2, 0, 1),
        "w_q": rows(L0_attn_Wq),
        "w_k": rows(L0_attn_Wk_up),
        "w_v": rows(L0_attn_Wv_up),
        "w_o_t": rows(np.asarray(L0_attn_Wo).T),
        "w_kvd": rows(np.asarray(L0_attn_Wkv_down).T),
    }
    arrays = {name: np.ascontiguousarray(a) for name, a in arrays.items()}
    nc = bacc.Bacc("TRN2", target_bir_lowering=False, num_devices=1)
    args = [nc.dram_tensor(name, a.shape, F32, kind="ExternalInput").ap() for name, a in arrays.items()]
    out = nc.dram_tensor("out", _OUT[0], F32, kind="ExternalOutput").ap()
    build(nc, *args, out)
    r = run_bass_kernel_spmd(nc, [arrays], core_ids=[0])
    return r.results[0]["out"]
```

```python
from contextlib import ExitStack

import concourse.bass as bass
from concourse import mybir
from concourse.alu_op_type import AluOpType as ALU

ACT = mybir.ActivationFunctionType
F32 = mybir.dt.float32
BF16 = mybir.dt.bfloat16
F32R = mybir.dt.float32r
I32 = mybir.dt.int32
AX_X = mybir.AxisListType.X
ds = bass.ds

P = 128
D = 256
DC = D // P
BATCH = 4
SEQ = 1024
TOK = BATCH * SEQ
NT = TOK // P
HEADS = 8
HD = 64
PAIRS = HEADS // 2
EXPERTS = 8
INNER = 128
SLOT_TILES = NT + EXPERTS
SLOTS = SLOT_TILES * P
EPS = 1e-5
SCALE = HD ** -0.5
HALF = 512
QT = SEQ // P
KT = SEQ // P
STEPS = 2 * KT
MAXES = 2 * QT * 2
LOADS = 4
LAG = 3
RING = 4
ROW_PAIRS = QT // 2
A_STEPS = (5, 7)
ROUTER_STEPS = ((0, 2), (0, 12), (0, 15), (1, 12), (1, 15), (2, 5), (2, 7), (2, 12), (2, 15), (3, 5), (3, 7), (3, 13))
EARLY = len(ROUTER_STEPS)
BACK = QT + ROW_PAIRS + 2
FOLD_O = (7, 4)
L_STEP = 15


def build(nc, x_in, gate_t, w_gu, w_dn, w_q, w_k, w_v, w_o_t, w_kvd, out):
    with ExitStack() as ctx:
        def sb(name, shape, dt=F32):
            return ctx.enter_context(nc.sbuf_tensor(name, shape, dt))

        sems = {}

        def sem(name):
            if name not in sems:
                sems[name] = ctx.enter_context(nc.semaphore(name))
            return sems[name]

        scaled_x = nc.dram_tensor("scaled_x", [TOK, D], F32, kind="Internal").ap()
        sorted_y = nc.dram_tensor("sorted_y", [SLOTS, D], F32, kind="Internal").ap()

        x_res = sb("x_res", [P, NT * D])
        arena_a = sb("arena_a", [P, DC * TOK])
        arena_b = sb("arena_b", [P, 8192])
        keys_next = sb("keys_next", [P, 2, SEQ], F32R)
        keys_now = sb("keys_now", [P, 2, SEQ], F32R)
        latent_next = sb("latent_next", [P, KT, HD])
        latent_now = sb("latent_now", [P, KT, HD])
        row_pairs = sb("row_pairs", [P, 2, 2 * D])
        q_split = sb("q_split", [P, PAIRS, 2, SEQ], F32R)
        q_shift = sb("q_shift", [P, 2, 2, SEQ], F32R)
        w_qk = sb("w_qk", [P, DC, PAIRS, P])
        w_vo = sb("w_vo", [P, PAIRS, D])
        ident = sb("ident", [P, P])
        before = sb("before", [P, P])
        ones = sb("ones", [P, P])
        gate_w = sb("gate_w", [P, DC, EXPERTS])
        kvd = sb("kvd", [P, DC, P])
        stats = sb("stats", [P, NT, 6])
        st = sb("st", [P, 8, NT])
        slots = sb("slots", [P, NT], I32)
        slot_row = sb("slot_row", [P, NT], I32)
        token_of = sb("token_of", [P, SLOT_TILES], I32)
        rows_store = sb("rows_store", [P, RING, 2 * D])
        hot_lo = sb("hot_lo", [P, NT, P], BF16)
        hot_hi = sb("hot_hi", [P, NT, SLOT_TILES], BF16)
        hot_id = sb("hot_id", [P, NT, 2, SLOT_TILES], BF16)
        count_p = sb("count_p", [P, P])
        row0 = sb("row0", [P, SLOT_TILES])
        my_p = sb("my_p", [P, 1])
        tile_experts = sb("tile_experts", [P, SLOT_TILES // RING + 1], I32)
        logits = sb("logits", [P, NT * EXPERTS])
        small = sb("small", [P, 8, EXPERTS])
        small_i = sb("small_i", [P, EXPERTS], I32)
        maxes = sb("maxes", [P, MAXES])
        top_q = sb("top_q", [P, 2 * QT])
        shift_q = sb("shift_q", [P, 4 * QT])
        shift_t = sb("shift_t", [4 * QT, P], F32R)

        xn_t = arena_a[:, :].rearrange("p (c n) -> p c n", c=DC)
        gu_sb = arena_a[:, 0:4096].rearrange("p (e c n) -> p e c n", e=EXPERTS, c=DC)
        dn_sb = arena_a[:, 4096:6144].rearrange("p (e n) -> p e n", e=EXPERTS)

        gu_split = q_split[:, :, :, :].rearrange("p a s n -> p (a s n)")
        dn_split = q_shift[:, :, :, :].rearrange("p b a n -> p (b a n)")
        rows_hi, rows_lo = (keys_now[:, 0, j * 2 * D:(j + 1) * 2 * D].rearrange("p (b n) -> p b n", b=2) for j in range(2))
        hid_hi, hid_lo = (keys_now[:, 1, j * 2 * INNER:(j + 1) * 2 * INNER].rearrange("p (b n) -> p b n", b=2)
                          for j in range(2))
        GU, DN = EXPERTS * DC * 2 * INNER, EXPERTS * D

        def route_tmp(n):
            return arena_a[:, 6144 + n * 256:6144 + (n + 1) * 256].rearrange("p (t e) -> p t e", e=EXPERTS)

        att_o = arena_b[:, 0:4096].rearrange("p (h n) -> p h n", h=PAIRS)
        prob = arena_b[:, 4096:6144].rearrange("p (b a n) -> p b a n", b=2, a=2)
        prob_sum = arena_b[:, 6144:8192].rearrange("p (b a n) -> p b a n", b=2, a=2)
        take_at = [0]

        def take(n, w):
            a = take_at[0]
            take_at[0] += n * w
            return arena_b[:, a:a + n * w].rearrange("p (b n) -> p b n", b=n)

        q_raw, k_raw, v_raw, o_raw = take(PAIRS, D), take(PAIRS, HD), take(PAIRS, HD), take(PAIRS, D)
        rows_back = take(RING, D)
        rows_in = take(RING, D)
        x_row, x_col = row_pairs, rows_store[:, 0:2, :]
        silu_g = take(2, INNER)
        hid = take(2, INNER)
        y_rows = take(RING, D)
        assert take_at[0] <= 8192

        ps = [ctx.enter_context(nc.psum_tensor(f"ps{i}", [P, 2, HALF], F32)) for i in range(3)]
        ps_o = ctx.enter_context(nc.psum_tensor("ps_o", [P, HALF], F32))
        ps_x = ctx.enter_context(nc.psum_tensor("ps_x", [P, HALF], F32))
        banks = [ps[i][:, j, :] for i in range(3) for j in range(2)] + [ps_o[:, :], ps_x[:, :]]
        ps_s = ps[0:2]
        ps_m = [ps[2][:, j, :] for j in range(2)]

        x_tiles = x_in.rearrange("b (t p) d -> p (b t) d", p=P)
        out_tiles = out.rearrange("b (t p) d -> p (b t) d", p=P)

        def x_tile(t):
            return x_res[:, ds(t * D, D)] if not isinstance(t, int) else x_res[:, t * D:(t + 1) * D]

        def each(eng, n, body):
            body(0, True)
            with eng.Fori(1, n) as i:
                body(i, False)

        block = ctx.enter_context(nc.Block())


        def pe_transposed(pe, tag):
            def logit(i, k):
                n = 2 * i + k
                pe.wait_ge(sem(f"col_ready_{tag}"), n + 1)
                for j in range(2):
                    for c in range(DC):
                        last = nc.tensor.matmul(banks[2][:, ds((2 * n + j) * EXPERTS, EXPERTS)],
                                                x_col[:, k, j * D + c * P:j * D + (c + 1) * P], gate_w[:, c, :],
                                                start=(c == 0), stop=(c == DC - 1))
                last.then_inc(sem(f"logit_{tag}"), 1)

            start = EARLY if tag == "f2" else 0

            def body(i, first):
                for k in range(2):
                    n = 2 * i + k
                    pe.wait_ge(sem(f"row_ready_{tag}"), 2 * n + 2)
                    if not first:
                        pe.wait_ge(sem(f"col_ready_{tag}"), n - 1)
                    for j in range(2):
                        for c in range(DC):
                            last = nc.tensor.transpose(banks[k][:, j * D + c * P:j * D + (c + 1) * P],
                                                       x_row[:, k, j * D + c * P:j * D + (c + 1) * P], ident[:, :])
                    last.then_inc(sem(f"row_turned_{tag}"), 1)
                    if k == 1:
                        logit(i, 0)
                    elif not first and not (isinstance(i, int) and 2 * i == start):
                        logit(i - 1, 1)
            if tag == "f1":
                each(pe, NT // 4, body)
            else:
                for i in range(start // 2, NT // 4):
                    body(i, False)
            logit(NT // 4 - 1, 1)

        def act_transposed(act, tag):
            def body(i, first, between=None):
                for k in range(2):
                    n = 2 * i + k
                    if k == 1 and between:
                        between()
                    act.wait_ge(sem(f"row_turned_{tag}"), n + 1)
                    if not first:
                        act.wait_ge(sem(f"logit_{tag}"), n - 1)
                    nc.scalar.activation(x_col[:, k, :], banks[k], ACT.Copy).then_inc(sem(f"col_ready_{tag}"), 1)
            if tag == "f1":
                n = NT // LOADS // 4
                for g in range(LOADS):
                    for i in range(n * g, n * (g + 1)):
                        def next_std():
                            act_std(act, "f1", (g + 1) * NT // LOADS, (g + 2) * NT // LOADS, g + 1)
                        body(i, i == 0, next_std if i == n * (g + 1) - 1 and g + 1 < LOADS else None)
            else:
                for i in range(EARLY // 2, NT // 4):
                    body(i, False)

        def dve_rows(dve, tag):
            def body(i, first):
                for k in range(2):
                    for j in range(2):
                        t = 4 * i + 2 * k + j
                        if not first and j == 0:
                            dve.wait_ge(sem(f"row_turned_{tag}"), 2 * i + k - 1)
                        nc.vector.tensor_scalar(x_row[:, k, j * D:(j + 1) * D], x_tile(t), st[:, 4, ds(t, 1)],
                                                st[:, 5, ds(t, 1)], ALU.mult, ALU.add) \
                            .then_inc(sem(f"row_ready_{tag}"), 1)
            if tag == "f1":
                def arrived(g):
                    dve.wait_ge(sem(f"x_loaded{g}"), 16)
                    with dve.Fori(g * NT // LOADS, (g + 1) * NT // LOADS) as t:
                        tile_stats(t, tag)
                arrived(0)
                for g in range(LOADS):
                    t0, t1 = g * NT // LOADS, (g + 1) * NT // LOADS
                    dve_stats(dve, tag, t0, t1, g)
                    for i in range(t0 // 4, t1 // 4):
                        body(i, i == 0)
                        if i == t0 // 4 and g + 1 < LOADS:
                            arrived(g + 1)
            else:
                dve_stats(dve, tag, 2 * EARLY, NT, 1)
                for i in range(EARLY // 2, NT // 4):
                    body(i, False)

        link_count = [0]

        def link(ins):
            link_count[0] += 1
            ins.then_inc(sem("dve_link"), 1)
            nc.vector.wait_ge(sem("dve_link"), link_count[0])

        def tile_stats(t, tag):
            nc.vector.bn_stats(stats[:, ds(t, 1), :], x_tile(t)).then_inc(sem(f"stats_{tag}"), 1)

        def dve_stats(dve, tag, t0, t1, part=0):
            dve_variance(dve, tag, t0, t1)
            dve_scale(dve, tag, t0, t1, part)

        def dve_variance(dve, tag, t0, t1):
            dve.wait_ge(sem(f"stats_{tag}"), t1)
            total, diff, var = (st[:, j, t0:t1] for j in range(3))
            half = stats[:, t0:t1, :]
            nc.vector.tensor_tensor(total, half[:, :, 1], half[:, :, 4], ALU.add)
            link(nc.vector.tensor_tensor(diff, half[:, :, 1], half[:, :, 4], ALU.subtract))
            nc.vector.tensor_tensor(var, half[:, :, 2], half[:, :, 5], ALU.add)
            link(nc.vector.tensor_tensor(diff, diff, diff, ALU.mult))
            link(nc.vector.tensor_scalar(var, var, 1.0 / D, EPS, ALU.mult, ALU.add))
            link(nc.vector.scalar_tensor_tensor(var, diff, 0.25, var, ALU.mult, ALU.add))
            nc.vector.tensor_copy(diff, var).then_inc(sem(f"var_{tag}"), 1)

        def dve_scale(dve, tag, t0, t1, part):
            total, diff, var, std, inv, shift = (st[:, j, t0:t1] for j in range(6))
            dve.wait_ge(sem(f"std_{tag}"), part + 1)
            link(nc.vector.reciprocal(inv, std))
            link(nc.vector.tensor_tensor(diff, inv, inv, ALU.mult))
            link(nc.vector.tensor_tensor(diff, diff, var, ALU.mult))
            link(nc.vector.tensor_scalar(diff, diff, -0.5, 1.5, ALU.mult, ALU.add))
            link(nc.vector.tensor_tensor(inv, inv, diff, ALU.mult))
            link(nc.vector.scalar_tensor_tensor(shift, total, -0.5, inv, ALU.mult, ALU.mult))

        def act_std(act, tag, t0=0, t1=NT, part=0):
            act.wait_ge(sem(f"var_{tag}"), part + 1)
            nc.scalar.activation(st[:, 3, t0:t1], st[:, 1, t0:t1], ACT.Sqrt).then_inc(sem(f"std_{tag}"), 1)


        def dve_route(dve, tag):
            top, rank, one_hot = st[:, 6, :], route_tmp(1), route_tmp(2)
            wide = [P, NT, EXPERTS]
            dve.wait_ge(sem(f"logit_{tag}"), NT // 2)
            lg = banks[2][:, 0:NT * EXPERTS]
            if tag == "f2":
                late = slice(2 * EARLY * EXPERTS, NT * EXPERTS)
                link(nc.vector.tensor_copy(logits[:, late], lg[:, late]))
                lg = logits[:, :]
            lg = lg.rearrange("p (t e) -> p t e", e=EXPERTS)
            link(nc.vector.tensor_reduce(top, lg, AX_X, ALU.max))
            nc.vector.tensor_copy(st[:, 7, :], top).then_inc(sem(f"top_{tag}"), 1)
            link(nc.vector.tensor_tensor(rank, lg, top.unsqueeze(2).to_broadcast(wide), ALU.is_equal))
            link(nc.vector.tensor_tensor(rank, rank, small[:, 7, :].unsqueeze(1).to_broadcast(wide), ALU.mult))
            link(nc.vector.tensor_reduce(top, rank, AX_X, ALU.max))
            link(nc.vector.tensor_tensor(one_hot, rank, top.unsqueeze(2).to_broadcast(wide), ALU.is_equal))
            nc.vector.tensor_copy(route_tmp(0), one_hot).then_inc(sem(f"one_hot_{tag}"), 1)
            dve.wait_ge(sem(f"exp_top_{tag}"), 1)
            link(nc.vector.tensor_scalar(st[:, 3, :], st[:, 3, :], 1.0, None, ALU.add))
            link(nc.vector.reciprocal(st[:, 3, :], st[:, 3, :]))
            nc.vector.tensor_tensor(st[:, 4, :], st[:, 4, :], st[:, 3, :], ALU.mult)
            nc.vector.tensor_tensor(st[:, 5, :], st[:, 5, :], st[:, 3, :], ALU.mult).then_inc(sem(f"scale_{tag}"), 1)
            dve.wait_ge(sem(f"ranks_{tag}"), 2)
            a, b = route_tmp(0), route_tmp(3)
            counts = banks[4][:, 0:NT * EXPERTS].rearrange("p (t e) -> p t e", e=EXPERTS)
            link(nc.vector.tensor_copy(a, counts))
            s = 1
            while s < NT:
                nc.vector.tensor_copy(b[:, 0:s, :], a[:, 0:s, :])
                link(nc.vector.tensor_tensor(b[:, s:NT, :], a[:, s:NT, :], a[:, 0:NT - s, :], ALU.add))
                a, b = b, a
                s *= 2
            n, up, end, base, tmp = (small[:, j, :] for j in range(5))
            link(nc.vector.tensor_scalar(n, a[:, NT - 1, :], float(P - 1), None, ALU.add))
            link(nc.vector.tensor_copy(small_i[:, :], n))
            link(nc.vector.tensor_scalar(small_i[:, :], small_i[:, :], 7, 7, ALU.logical_shift_right,
                                         ALU.logical_shift_left))
            link(nc.vector.tensor_copy(up, small_i[:, :]))
            link(nc.vector.tensor_copy(end, up))
            s, u, v = 1, end, tmp
            while s < EXPERTS:
                nc.vector.tensor_copy(v[:, 0:s], u[:, 0:s])
                link(nc.vector.tensor_tensor(v[:, s:EXPERTS], u[:, s:EXPERTS], u[:, 0:EXPERTS - s], ALU.add))
                u, v = v, u
                s *= 2
            link(nc.vector.tensor_tensor(base, u, up, ALU.subtract))
            within = banks[3][:, 0:NT * EXPERTS].rearrange("p (t e) -> p t e", e=EXPERTS)
            link(nc.vector.tensor_tensor(a, a, counts, ALU.subtract))
            link(nc.vector.tensor_tensor(a, a, within, ALU.add))
            link(nc.vector.tensor_tensor(a, a, base.unsqueeze(1).to_broadcast(wide), ALU.add))
            link(nc.vector.tensor_tensor(a, a, one_hot, ALU.mult))
            link(nc.vector.tensor_reduce(top, a, AX_X, ALU.add))
            link(nc.vector.tensor_copy(slots[:, :], top))
            at_row, lo = st[:, 1, :], st[:, 2, :]
            link(nc.vector.tensor_scalar(slot_row[:, :], slots[:, :], 7, 7, ALU.logical_shift_right,
                                         ALU.logical_shift_left))
            link(nc.vector.tensor_copy(at_row, slot_row[:, :]))
            highs = [P, NT, SLOT_TILES]
            nc.vector.tensor_tensor(hot_hi[:, :, :], at_row.unsqueeze(2).to_broadcast(highs),
                                    row0[:, :].unsqueeze(1).to_broadcast(highs), ALU.is_equal) \
                .then_inc(sem(f"hot_hi_{tag}"), 1)
            link(nc.vector.tensor_tensor(lo, top, at_row, ALU.subtract))
            for g in range(RING):
                ts = slice(g * NT // RING, (g + 1) * NT // RING)
                lows = [P, NT // RING, P]
                nc.vector.tensor_tensor(hot_lo[:, ts, :], lo[:, ts].unsqueeze(2).to_broadcast(lows),
                                        count_p[:, :].unsqueeze(1).to_broadcast(lows), ALU.is_equal) \
                    .then_inc(sem(f"hot_lo_{tag}"), 1)
                if g == 0:
                    dve.wait_ge(sem(f"hot_hi_{tag}"), 1)
                    nc.vector.tensor_tensor(hot_id[:, :, 0, :], hot_hi[:, :, :],
                                            count_p[:, 0:NT].unsqueeze(2).to_broadcast(highs), ALU.mult) \
                        .then_inc(sem(f"hot_id_{tag}"), 1)
            dve.wait_ge(sem(f"tokens_{tag}"), 1)
            parts = banks[5][:, 0:2 * SLOT_TILES].rearrange("p (a h) -> p a h", a=2)
            in_tile, ids = route_tmp(0)[:, 0:5, :], route_tmp(3)[:, 0:5, :]
            in_tile, ids = (v.rearrange("p t e -> p (t e)") for v in (in_tile, ids))
            link(nc.vector.tensor_copy(in_tile, parts[:, 1, :]))
            link(nc.vector.scalar_tensor_tensor(ids, parts[:, 0, :], float(P), in_tile, ALU.mult, ALU.add))
            nc.vector.tensor_copy(token_of[:, :], ids).then_inc(sem(f"token_of_{tag}"), 1)
            return u

        def dve_tile_experts(dve, tag, ends):
            tiles = [P, SLOT_TILES, EXPERTS]
            cmp_a = arena_a[:, 6144 + 1024:6144 + 1024 + SLOT_TILES * EXPERTS].rearrange("p (t e) -> p t e", e=EXPERTS)
            padded = arena_a[:, 6144 + 1450:6144 + 1450 + SLOT_TILES + RING + LAG]
            cnt = padded[:, LAG:LAG + SLOT_TILES]
            code = arena_a[:, 6144 + 1500:6144 + 1500 + SLOT_TILES // RING + 1]
            nc.vector.memset(padded[:, 0:LAG], 0.0)
            nc.vector.memset(padded[:, LAG + SLOT_TILES:], 0.0)
            link(nc.vector.tensor_tensor(cmp_a, ends.unsqueeze(1).to_broadcast(tiles),
                                         row0[:, :].unsqueeze(2).to_broadcast(tiles), ALU.is_le))
            link(nc.vector.tensor_reduce(cnt, cmp_a, AX_X, ALU.add))
            link(nc.vector.tensor_scalar(cnt, cnt, float(EXPERTS - 1), None, ALU.min))

            def digit(j):
                return padded[:, j:j + SLOT_TILES + 1:RING]
            link(nc.vector.tensor_copy(code, digit(RING + LAG - 1)))
            for j in range(RING + LAG - 2, -1, -1):
                link(nc.vector.scalar_tensor_tensor(code, code, float(EXPERTS), digit(j), ALU.mult, ALU.add))
            nc.vector.tensor_copy(tile_experts[:, :], code).then_inc(sem(f"tile_expert_{tag}"), 1)

        def pe_tokens(pe, tag):
            pe.wait_ge(sem(f"hot_id_{tag}"), 2)
            for t in range(NT):
                if t % (NT // RING) == 0:
                    pe.wait_ge(sem(f"hot_lo_{tag}"), t // (NT // RING) + 1)
                last = nc.tensor.matmul(banks[5][:, 0:2 * SLOT_TILES], hot_lo[:, t, :],
                                        hot_id[:, t, :, :].rearrange("p a h -> p (a h)"),
                                        start=(t == 0), stop=(t == NT - 1))
            last.then_inc(sem(f"tokens_{tag}"), 1)

        def act_hot_id(act, tag):
            act.wait_ge(sem(f"hot_hi_{tag}"), 1)
            nc.scalar.activation(hot_id[:, :, 1, :], hot_hi[:, :, :], ACT.Copy, scale=my_p[:, 0:1]) \
                .then_inc(sem(f"hot_id_{tag}"), 1)

        def pe_ranks(pe, tag):
            pe.wait_ge(sem(f"one_hot_{tag}"), 1)
            hot = route_tmp(0).rearrange("p t e -> p (t e)")
            nc.tensor.matmul(banks[3][:, 0:NT * EXPERTS], before[:, :], hot, start=True, stop=True) \
                .then_inc(sem(f"ranks_{tag}"), 1)
            nc.tensor.matmul(banks[4][:, 0:NT * EXPERTS], ones[:, :], hot, start=True, stop=True) \
                .then_inc(sem(f"ranks_{tag}"), 1)

        def act_exp_top(act, tag):
            act.wait_ge(sem(f"top_{tag}"), 1)
            nc.scalar.activation(st[:, 3, :], st[:, 7, :], ACT.Exp, scale=-1.0).then_inc(sem(f"exp_top_{tag}"), 1)

        def act_scaled_rows(act, tag):
            act.wait_ge(sem(f"scale_{tag}"), 1)

            def body(i, first):
                for k in range(RING):
                    if not first:
                        act.wait_ge(sem(f"stored{k}_{tag}"), 16 * i)
                    for j in range(2):
                        t = 2 * (RING * i + k) + j
                        nc.scalar.activation(rows_store[:, k, j * D:(j + 1) * D], x_tile(t), ACT.Identity,
                                             bias=st[:, 5, ds(t, 1)], scale=st[:, 4, ds(t, 1)]) \
                            .then_inc(sem(f"scaled_{tag}"), 1)
            last = NT // (2 * RING) - 1
            body(0, True)
            with act.Fori(1, last) as i:
                body(i, False)
            act_hot_id(act, tag)
            body(last, False)

        def sp_scaled_rows(sp, tag):
            def body(i, first):
                for k in range(RING):
                    n = RING * i + k
                    row = n * 2 * P if first else sp.snap(n * 2 * P)
                    sp.wait_ge(sem(f"scaled_{tag}"), 2 * n + 2)
                    sp.dma_start(scaled_x[ds(row, 2 * P), :].rearrange("(j p) d -> p j d", j=2),
                                 rows_store[:, k, :].rearrange("p (j d) -> p j d", j=2)) \
                        .then_inc(sem(f"stored{k}_{tag}"), 16)
            body(0, True)
            with sp.Fori(1, NT // (2 * RING)) as i:
                body(i, False)

        def pool_split_weights(pool, tag):
            pool.wait_ge(sem(f"experts_loaded_{tag}"), 32)
            done = 0
            for src, dst, width in ((arena_a[:, 0:GU], gu_split, GU), (arena_a[:, GU:GU + DN], dn_split, DN)):
                for a in range(0, width, SEQ):
                    done += 1
                    hi = dst[:, a:a + SEQ]
                    nc.gpsimd.tensor_copy(hi, src[:, a:a + SEQ]).then_inc(sem(f"weights_hi_{tag}"), 1)
                    pool.wait_ge(sem(f"weights_hi_{tag}"), done)
                    nc.gpsimd.tensor_tensor(dst[:, width + a:width + a + SEQ], src[:, a:a + SEQ], hi.bitcast(F32),
                                            ALU.subtract).then_inc(sem(f"weights_split_{tag}"), 1)

        def pool_sorted_rows(pool, tag):
            for k in range(RING):
                pool.wait_ge(sem(f"stored{k}_{tag}"), 16 * (NT // (2 * RING)))
            pool.wait_ge(sem(f"token_of_{tag}"), 1)
            for t in range(SLOT_TILES):
                k = t % RING
                if t >= RING:
                    pool.wait_ge(sem(f"in_turned_{tag}"), t - RING + 1)
                pool.indirect_dma_start(rows_in[:, k, :], None, scaled_x[:, :],
                                        bass.IndirectOffsetOnAxis(ap=token_of[:, t:t + 1], axis=0)) \
                    .then_inc(sem(f"in{k}_{tag}"), 16)

        def old(t, n):
            return not isinstance(t, int) or t >= n

        def in_range(t):
            return not isinstance(t, int) or 0 <= t < SLOT_TILES

        def expert_tiles(eng, tile):
            for t in range(RING):
                tile(t, t % RING, False)
            with eng.Fori(0, (SLOT_TILES // RING - 2) // 2) as i:
                for h in range(2):
                    for k in range(RING):
                        tile(2 * RING * i + RING * (h + 1) + k, k, h == 0)
            for t in range(SLOT_TILES - RING, SLOT_TILES + LAG + 1):
                tile(t, t % RING, t < SLOT_TILES)

        def pe_experts(pe, tag):
            def turn(t, k):
                pe.wait_ge(sem(f"in{k}_{tag}"), 16 * (t // RING + 1) if isinstance(t, int) else (t - k) * 4 + 16)
                if old(t, 2):
                    pe.wait_ge(sem(f"rows_lo_{tag}"), t - 1)
                for c in range(DC):
                    last = nc.tensor.transpose(banks[k % 2][:, c * P:(c + 1) * P], rows_in[:, k, c * P:(c + 1) * P],
                                               ident[:, :])
                last.then_inc(sem(f"in_turned_{tag}"), 1)

            digits, ready = [], []

            def load_experts(group):
                code = pe.value_load(tile_experts[0:1, ds(group, 1)], min_val=0, max_val=EXPERTS ** (RING + LAG) - 1)
                ready.append([code // EXPERTS ** j % EXPERTS for j in range(RING + LAG)])

            def gate_up(t, k, e):
                pe.wait_ge(sem(f"rows_lo_{tag}"), t + 1)
                if old(t, 2):
                    pe.wait_ge(sem(f"hid_{tag}"), t - 1)
                for c in range(DC):
                    for rows, part in ((rows_hi, 0), (rows_hi, GU), (rows_lo, 0)):
                        last = nc.tensor.matmul(banks[2 + k % 2][:, 0:2 * INNER],
                                                rows[:, k % 2, c * P:(c + 1) * P],
                                                gu_split[:, ds(e * (DC * 2 * INNER) + (c * 2 * INNER + part), 2 * INNER)],
                                                start=(c == 0 and rows is rows_hi and part == 0),
                                                stop=(c == DC - 1 and rows is rows_lo))
                last.then_inc(sem(f"gate_up_{tag}"), 1)

            def turn_hidden(t, k):
                pe.wait_ge(sem(f"hid_{tag}"), t + 1)
                if old(t, 2):
                    pe.wait_ge(sem(f"hid_lo_{tag}"), t - 1)
                nc.tensor.transpose(banks[4 + k % 2][:, 0:P], hid[:, k % 2, :], ident[:, :]) \
                    .then_inc(sem(f"hid_turned_{tag}"), 1)

            def down(t, k, e):
                pe.wait_ge(sem(f"hid_lo_{tag}"), t + 1)
                if old(t, 2):
                    pe.wait_ge(sem(f"y_ready_{tag}"), t - 1)
                for hidden, part in ((hid_hi, 0), (hid_hi, DN), (hid_lo, 0)):
                    last = nc.tensor.matmul(banks[6 + k % 2][:, 0:D], hidden[:, k % 2, :],
                                            dn_split[:, ds(e * D + part, D)],
                                            start=(hidden is hid_hi and part == 0), stop=(hidden is hid_lo))
                last.then_inc(sem(f"down_{tag}"), 1)

            def tile(t, k, ahead):
                if k == 0 and not ready:
                    load_experts(t // RING)
                if k == 0:
                    digits[:] = ready.pop()
                if in_range(t):
                    gate_up(t, k, digits[k + LAG])
                if in_range(t - LAG):
                    down(t - LAG, (k - LAG) % RING, digits[k])
                if k == 2 and ahead:
                    load_experts(t // RING + 1)
                if in_range(t + 2):
                    turn(t + 2, (k + 2) % RING)
                if in_range(t - 1):
                    turn_hidden(t - 1, (k - 1) % RING)
            pe.wait_ge(sem(f"weights_split_{tag}"), (GU + DN) // SEQ)
            pe.wait_ge(sem(f"tile_expert_{tag}"), 1)
            turn(0, 0)
            turn(1, 1)
            expert_tiles(pe, tile)

        def act_experts(act, tag):
            def copy_in(t, k):
                act.wait_ge(sem(f"in_turned_{tag}"), t + 1)
                if old(t, 2):
                    act.wait_ge(sem(f"gate_up_{tag}"), t - 1)
                nc.scalar.activation(rows_hi[:, k % 2, :], banks[k % 2][:, 0:D], ACT.Copy) \
                    .then_inc(sem(f"rows_hi_{tag}"), 1)

            def copy_hidden(t, k):
                act.wait_ge(sem(f"hid_turned_{tag}"), t + 1)
                if old(t, 2):
                    act.wait_ge(sem(f"down_{tag}"), t - 1)
                nc.scalar.activation(hid_hi[:, k % 2, :], banks[4 + k % 2][:, 0:P], ACT.Copy) \
                    .then_inc(sem(f"hid_hi_{tag}"), 1)

            def y_out(t, k):
                act.wait_ge(sem(f"down_{tag}"), t + 1)
                if old(t, RING):
                    act.wait_ge(sem(f"y_stored{k}_{tag}"), 16 * (t // RING) if isinstance(t, int) else (t - k) * 4)
                nc.scalar.activation(y_rows[:, k, :], banks[6 + k % 2][:, 0:D], ACT.Copy) \
                    .then_inc(sem(f"y_ready_{tag}"), 1)

            def silu(t, k):
                act.wait_ge(sem(f"gate_up_{tag}"), t + 1)
                if old(t, 2):
                    act.wait_ge(sem(f"hid_{tag}"), t - 1)
                nc.scalar.activation(silu_g[:, k % 2, :], banks[2 + k % 2][:, 0:INNER], ACT.Silu) \
                    .then_inc(sem(f"silu_{tag}"), 1)

            def store(t, k):
                row = t * P if isinstance(t, int) else act.snap(t * P)
                act.wait_ge(sem(f"y_ready_{tag}"), t + 1)
                act.dma_start(sorted_y[ds(row, P), :], y_rows[:, k, :]).then_inc(sem(f"y_stored{k}_{tag}"), 16)

            def tile(t, k, ahead):
                if in_range(t):
                    silu(t, k)
                if in_range(t - LAG):
                    y_out(t - LAG, (k - LAG) % RING)
                if in_range(t + 2):
                    copy_in(t + 2, (k + 2) % RING)
                if in_range(t - 1):
                    copy_hidden(t - 1, (k - 1) % RING)
                if in_range(t - LAG - 1):
                    store(t - LAG - 1, (k - LAG - 1) % RING)
            copy_in(0, 0)
            copy_in(1, 1)
            expert_tiles(act, tile)

        def dve_experts(dve, tag):
            def rows_rest(t, k):
                dve.wait_ge(sem(f"rows_hi_{tag}"), t + 1)
                nc.vector.tensor_tensor(rows_lo[:, k % 2, :], banks[k % 2][:, 0:D],
                                        rows_hi[:, k % 2, :].bitcast(F32),
                                        ALU.subtract).then_inc(sem(f"rows_lo_{tag}"), 1)

            def hidden_rest(t, k):
                dve.wait_ge(sem(f"hid_hi_{tag}"), t + 1)
                nc.vector.tensor_tensor(hid_lo[:, k % 2, :], banks[4 + k % 2][:, 0:P],
                                        hid_hi[:, k % 2, :].bitcast(F32), ALU.subtract).then_inc(sem(f"hid_lo_{tag}"), 1)

            def gated(t, k):
                dve.wait_ge(sem(f"silu_{tag}"), t + 1)
                if old(t, 2):
                    dve.wait_ge(sem(f"hid_turned_{tag}"), t - 1)
                nc.vector.tensor_tensor(hid[:, k % 2, :], silu_g[:, k % 2, :], banks[2 + k % 2][:, INNER:2 * INNER],
                                        ALU.mult).then_inc(sem(f"hid_{tag}"), 1)

            def tile(t, k, ahead):
                if in_range(t):
                    gated(t, k)
                if in_range(t + 2):
                    rows_rest(t + 2, (k + 2) % RING)
                if in_range(t - 1):
                    hidden_rest(t - 1, (k - 1) % RING)
            rows_rest(0, 0)
            rows_rest(1, 1)
            expert_tiles(dve, tile)

        def pool_gather(pool, tag):
            for k in range(RING):
                pool.wait_ge(sem(f"y_stored{k}_{tag}"), 16 * (SLOT_TILES // RING))
            for t in range(NT):
                k = t % RING
                if t >= RING:
                    pool.wait_ge(sem(f"ffn_added_{tag}"), t - RING + 1)
                if tag == "f1" and t == NT // 2:
                    pool.memset(q_shift[HD:P, :, :, :].bitcast(F32), 0.0).then_inc(sem("q_fill"), 1)
                pool.indirect_dma_start(rows_back[:, k, :], None, sorted_y[:, :],
                                        bass.IndirectOffsetOnAxis(ap=slots[:, t:t + 1], axis=0)) \
                    .then_inc(sem(f"gathered{k}_{tag}"), 16)

        def dve_gathered(dve, tag, i, k):
            t = RING * i + k
            dve.wait_ge(sem(f"gathered{k}_{tag}"), 16 * i + 16)
            nc.vector.scalar_tensor_tensor(x_tile(t), rows_back[:, k, :], 0.5, x_tile(t),
                                           ALU.mult, ALU.add).then_inc(sem(f"ffn_added_{tag}"), 1)
            if tag == "f1":
                dve.wait_ge(sem(f"ffn_added_{tag}"), t + 1)
                tile_stats(t, "att")

        def dve_gather(dve):
            with dve.Fori(0, NT // RING) as i:
                for k in range(RING):
                    dve_gathered(dve, "f2", i, k)
            dve.wait_ge(sem("ffn_added_f2"), NT)


        def pe_queries(pe, slot, c, tokens, bank):
            for d in range(DC):
                last = nc.tensor.matmul(bank, w_qk[:, d, slot, :], xn_t[:, d, ds(tokens, HALF)],
                                        start=(d == 0), stop=(d == DC - 1))
            last.then_inc(sem("q_made"), 1)

        def act_queries(act, slot, c, n, bank):
            act.wait_ge(sem("q_made"), n + 1)
            for a in range(2):
                nc.scalar.activation(q_split[0:HD, slot, a, c * HALF:(c + 1) * HALF], bank[a * HD:(a + 1) * HD, :],
                                     ACT.Copy).then_inc(sem("q_hi"), 1)

        def dve_queries(dve, slot, c, a, n, bank):
            dve.wait_ge(sem("q_hi"), 2 * n + a + 1)
            nc.vector.tensor_tensor(q_split[HD:P, slot, a, c * HALF:(c + 1) * HALF], bank[a * HD:(a + 1) * HD, :],
                                    q_split[0:HD, slot, a, c * HALF:(c + 1) * HALF].bitcast(F32), ALU.subtract) \
                .then_inc(sem("q_lo"), 1)

        def pe_max(pe, slot, m, keys, n, first):
            a, qt, half = m // (2 * QT), m // 2 % QT, m % 2
            if not first:
                pe.wait_ge(sem("max_taken"), n - 1)
            nc.tensor.matmul(ps_m[m % 2], q_split[:, slot, a, qt * P:(qt + 1) * P],
                             keys[:, 0, half * HALF:(half + 1) * HALF], start=True, stop=True) \
                .then_inc(sem("max_scores"), 1)

        def dve_max(dve, m, n):
            dve.wait_ge(sem("max_scores"), n + 1)
            nc.vector.tensor_reduce(maxes[:, m:m + 1], ps_m[m % 2], AX_X, ALU.max).then_inc(sem("max_taken"), 1)

        def dve_shift(dve, n, u):
            dve.wait_ge(sem("max_taken"), n)
            pairs = maxes[:, :].rearrange("p (q h) -> p q h", h=2)
            hi = shift_q[:, :].rearrange("p (a s q) -> p a s q", a=2, s=2)
            nc.vector.tensor_tensor(top_q[:, :], pairs[:, :, 0], pairs[:, :, 1], ALU.max) \
                .then_inc(sem("shift_top"), 1)
            dve.wait_ge(sem("shift_top"), u + 1)
            top = top_q[:, :].rearrange("p (a q) -> p a q", a=2)
            if not isinstance(u, int) or u > 0:
                dve.wait_ge(sem("shift_turned"), u)
            nc.vector.tensor_scalar(hi[:, :, 0, :].bitcast(F32R), top, -1.0, None, ALU.mult) \
                .then_inc(sem("shift_hi"), 1)
            dve.wait_ge(sem("shift_hi"), u + 1)
            nc.vector.scalar_tensor_tensor(hi[:, :, 1, :].bitcast(F32R), top, -1.0, hi[:, :, 0, :],
                                           ALU.mult, ALU.subtract).then_inc(sem("shift_lo"), 1)

        def pe_shift(pe, u):
            pe.wait_ge(sem("shift_lo"), u + 1)
            nc.tensor.transpose(ps_x[0:4 * QT, 0:P], shift_q[:, :], ident[:, :]).then_inc(sem("shift_turned"), 1)

        def act_shift(act, u, b=None, p=None):
            act.wait_ge(sem("shift_turned"), u + 1)
            if b is not None:
                act.wait_ge(sem(f"shift_placed{p % 2}"), 32 * (2 * b + p // 2 + 1))
            nc.scalar.activation(shift_t[:, :], ps_x[0:4 * QT, 0:P], ACT.Copy).then_inc(sem("shift_copied"), 1)

        def sp_shift(sp, slot, u):
            sp.wait_ge(sem("shift_copied"), u + 1)
            for a in range(2):
                sp.dma_start(q_shift[HD:HD + 2, slot % 2, a, :].bitcast(F32),
                             shift_t[2 * QT * a:2 * QT * (a + 1), :].bitcast(F32)).then_inc(sem(f"shift_placed{slot % 2}"), 16)

        def sp_queries(sp, slot):
            sp.dma_start(q_shift[0:HD, slot % 2, :, :].bitcast(F32), q_split[0:HD, slot, :, :].bitcast(F32)).then_inc(sem(f"q_copied{slot % 2}"), 16)

        def dve_norm_rows(dve, nb, i):
            n = ROW_PAIRS * nb + i
            if not isinstance(n, int) or n >= 2:
                dve.wait_ge(sem("rows_turned"), n - 1)
            for j in range(2):
                t = QT * nb + 2 * i + j
                nc.vector.tensor_scalar(row_pairs[:, i % 2, j * D:(j + 1) * D], x_tile(t), st[:, 4, ds(t, 1)],
                                        st[:, 5, ds(t, 1)], ALU.mult, ALU.add).then_inc(sem("rows_ready"), 1)

        def pe_turn_rows(pe, nb, i, bank):
            n = ROW_PAIRS * nb + i
            pe.wait_ge(sem("rows_ready"), 2 * n + 2)
            for g in range(4):
                last = nc.tensor.transpose(bank[:, g * P:(g + 1) * P], row_pairs[:, i % 2, g * P:(g + 1) * P],
                                           ident[:, :])
            last.then_inc(sem("rows_turned"), 1)

        def act_columns(act, nb, i, bank):
            act.wait_ge(sem("rows_turned"), ROW_PAIRS * nb + i + 1)
            nc.scalar.activation(
                xn_t[:, :, ds(nb * SEQ + i * 2 * P, 2 * P)].rearrange("p c (j n) -> p c j n", j=2),
                bank.rearrange("p (j c n) -> p c j n", j=2, c=DC), ACT.Copy).then_inc(sem("columns_ready"), 1)

        def pe_latents(pe, nb, j, bank):
            for d in range(DC):
                last = nc.tensor.matmul(bank, kvd[:, d, :], xn_t[:, d, ds(nb * SEQ + j * HALF, HALF)],
                                        start=(d == 0), stop=(d == DC - 1))
            last.then_inc(sem("lat_made"), 1)

        def act_latents(act, nb, j, bank):
            act.wait_ge(sem("lat_made"), 2 * nb + j + 1)
            nc.scalar.activation(row_pairs[:, j, :], bank, ACT.Copy).then_inc(sem("lat_f"), 1)
            nc.scalar.activation(keys_next[:, 0, j * HALF:(j + 1) * HALF], bank, ACT.Copy).then_inc(sem("lat_hi"), 1)

        def dve_keys_lo(dve, nb, j, bank):
            cols = slice(j * HALF, (j + 1) * HALF)
            dve.wait_ge(sem("lat_hi"), 2 * nb + j + 1)
            nc.vector.tensor_tensor(keys_next[0:HD, 1, cols], bank[0:HD, :],
                                    keys_next[0:HD, 0, cols].bitcast(F32), ALU.subtract).then_inc(sem("lat_lo"), 1)

        def pe_turn_latents(pe, nb, j, bank):
            pe.wait_ge(sem("lat_f"), 2 * nb + j + 1)
            pe.wait_ge(sem("lat_lo"), 2 * nb + j + 1)
            for g in range(4):
                last = nc.tensor.transpose(bank[:, g * P:(g + 1) * P], row_pairs[:, j, g * P:(g + 1) * P],
                                           ident[:, :])
            last.then_inc(sem("lat_turned"), 1)

        def dve_latent_rows(dve, nb, j, bank):
            dve.wait_ge(sem("lat_turned"), 2 * nb + j + 1)
            nc.vector.tensor_copy(latent_next[:, 4 * j:4 * j + 4, :],
                                  bank.rearrange("p (g n) -> p g n", g=4)[:, :, 0:HD]).then_inc(sem("lat_rows"), 1)

        def max_at(s):
            return sum((3, 3, 3, 1, 1, 3, 2, 3, 3, 3, 1, 1, 3, 2)[:s])

        def dve_early_rows(dve, n):
            if n >= 2:
                dve.wait_ge(sem("row_turned_f2"), n - 1)
            for j in range(2):
                t = 2 * n + j
                nc.vector.tensor_scalar(x_row[:, n % 2, j * D:(j + 1) * D], x_tile(t), st[:, 4, t:t + 1],
                                        st[:, 5, t:t + 1], ALU.mult, ALU.add).then_inc(sem("row_ready_f2"), 1)

        def pe_early_turn(pe, n):
            pe.wait_ge(sem("row_ready_f2"), 2 * n + 2)
            if n:
                pe.wait_ge(sem("logit_kept"), n)
            for g in range(4):
                last = nc.tensor.transpose(ps_x[:, g * P:(g + 1) * P], x_row[:, n % 2, g * P:(g + 1) * P], ident[:, :])
            last.then_inc(sem("row_turned_f2"), 1)

        def act_early_columns(act, n):
            act.wait_ge(sem("row_turned_f2"), n + 1)
            if n >= 2:
                act.wait_ge(sem("logit_f2"), n - 1)
            nc.scalar.activation(x_col[:, n % 2, :], ps_x[:, :], ACT.Copy).then_inc(sem("col_ready_f2"), 1)

        def pe_early_logits(pe, n):
            pe.wait_ge(sem("col_ready_f2"), n + 1)
            for j in range(2):
                for c in range(DC):
                    last = nc.tensor.matmul(ps_x[:, j * EXPERTS:(j + 1) * EXPERTS],
                                            x_col[:, n % 2, j * D + c * P:j * D + (c + 1) * P], gate_w[:, c, :],
                                            start=(c == 0), stop=(c == DC - 1))
            last.then_inc(sem("logit_f2"), 1)

        def dve_keep_logits(dve, n):
            dve.wait_ge(sem("logit_f2"), n + 1)
            nc.vector.tensor_copy(logits[:, 2 * n * EXPERTS:2 * (n + 1) * EXPERTS], ps_x[:, 0:2 * EXPERTS]) \
                .then_inc(sem("logit_kept"), 1)

        def router_pair(p, s, lag):
            at = STEPS * p + s - lag
            return ROUTER_STEPS.index((at // STEPS, at % STEPS)) if (at // STEPS, at % STEPS) in ROUTER_STEPS else None

        STEP_B = PAIRS * STEPS
        SUM_B = PAIRS * 2 * (KT - 1)

        def pe_attention(pe):
            for i in range(ROW_PAIRS):
                pe_turn_rows(pe, 0, i, banks[i])
            pe.wait_ge(sem("columns_ready"), ROW_PAIRS)
            for j in range(2):
                pe_latents(pe, 0, j, banks[4 + j])
            for j in range(2):
                pe_turn_latents(pe, 0, j, banks[4 + j])
            for n in range(4):
                pe_queries(pe, n // 2, n % 2, (n % 2) * HALF, banks[n])
            pe.wait_ge(sem("q_lo"), 4)
            pe.wait_ge(sem("lat_rows"), 2)
            for m in range(MAXES):
                pe_max(pe, 0, m, keys_next, m, m < 2)
            pe.wait_ge(sem("q_lo"), 8)
            pe_shift(pe, 0)
            pe.wait_ge(sem("batch_ready"), 32)
            pe.wait_ge(sem("keys_fill"), 1)
            pe.wait_ge(sem("q_fill"), 1)

            def batch(b):
                last_batch = isinstance(b, int)

                def max_next(p):
                    return not (last_batch and p == PAIRS - 1)

                def queries_next(p):
                    return not (last_batch and p >= PAIRS - 2)


                def scores(p, s, a):
                    c, kt = s // KT, s % KT
                    n = p * STEPS + s
                    if n == 0 and a == 0:
                        pe.wait_ge(sem("batch_ready"), 32 * b + 32)
                    if n >= 2 and a == 0:
                        pe.wait_ge(sem("exp_done"), STEP_B * b + n - 1)
                    if s == 0 and a == 0:
                        pe.wait_ge(sem(f"q_copied{p % 2}"), 16 * (2 * b + p // 2 + 1))
                        pe.wait_ge(sem(f"shift_placed{p % 2}"), 32 * (2 * b + p // 2 + 1))
                    o = ps_s[n % 2][:, a, :]
                    q = slice(c * HALF, (c + 1) * HALF)
                    k = slice(kt * P, (kt + 1) * P)
                    nc.tensor.matmul(o, keys_now[:, 0, k], q_split[:, p, a, q], start=True, stop=False)
                    last = nc.tensor.matmul(o, keys_now[:, 1, k], q_shift[:, p % 2, a, q], start=False, stop=True)
                    if a == 1:
                        last.then_inc(sem("scored"), 1)

                def values(p, s):
                    c, kt = s // KT, s % KT
                    n = p * STEPS + s
                    pe.wait_ge(sem("exp_done"), STEP_B * b + n + 1)
                    if kt == 0 and p + c:
                        pe.wait_ge(sem("o_copied"), 2 * PAIRS * b + 2 * p + c)
                    for a in range(2):
                        src = prob_sum[:, c, a, :] if kt == 0 else prob[:, kt % 2, a, :]
                        last = nc.tensor.matmul(ps_o[a * HD:(a + 1) * HD, :], latent_now[:, kt, :], src,
                                                start=(kt == 0), stop=(kt == KT - 1))
                    last.then_inc(sem("valued"), 1)

                made = [0]

                def logits_kept():
                    if made[0]:
                        pe.wait_ge(sem("logit_kept"), made[0])

                def denominators(p, c):
                    logits_kept()
                    pe.wait_ge(sem("summed"), SUM_B * b + (2 * p + c + 1) * (KT - 1))
                    for a in range(2):
                        last = nc.tensor.matmul(ps_x[a * HD:(a + 1) * HD, :], ones[:, 0:HD], prob_sum[:, c, a, :],
                                                start=True, stop=True)
                    last.then_inc(sem("denoms"), 1)

                for p in range(PAIRS):
                    wrap_m, wrap_a = p == PAIRS - 1, p >= PAIRS - 2
                    for s in range(STEPS):
                        todo = list(range(max_at(s), max_at(s + 1))) if max_next(p) else []

                        def piece():
                            if todo:
                                m = todo.pop(0)
                                if m == 0:
                                    pe.wait_ge(sem("q_lo"), 4 * PAIRS * b + 4 * (p + 1) + 4)
                                pe_max(pe, (p + 1) % PAIRS, m, keys_next if wrap_m else keys_now,
                                       MAXES * PAIRS * b + MAXES * (p + 1) + m, False)
                        scores(p, s, 0)
                        piece()
                        if s == 14 and max_next(p):
                            pe.wait_ge(sem("normed"), 4 * PAIRS * b + 4 * p + 2)
                            logits_kept()
                            pe_shift(pe, PAIRS * b + p + 1)
                        scores(p, s, 1)
                        piece()
                        if p or s:
                            values(p - (s == 0), (s - 1) % STEPS)
                        piece()
                        if p and s == 2:
                            pe.wait_ge(sem("shift_copied"), PAIRS * b + p + 1)
                            if not last_batch and p < 3:
                                pe.wait_ge(sem("lat_rows"), 2 * (b + 1) + p)
                            denominators(p - 1, 1)
                        if s in A_STEPS and queries_next(p):
                            c = A_STEPS.index(s)
                            n = 2 * PAIRS * b + 2 * (p + 2) + c
                            pe.wait_ge(sem("q_lo"), 2 * n)
                            logits_kept()
                            if p == 0 and not last_batch:
                                pe.wait_ge(sem("columns_ready"), ROW_PAIRS * (b + 2))
                            if p:
                                pe.wait_ge(sem("normed"), 4 * PAIRS * b + 4 * p)
                            pe_queries(pe, (p + 2) % PAIRS, c, (b + 1 if wrap_a else b) * SEQ + c * HALF, ps_x[:, :])
                        if last_batch:
                            n = router_pair(p, s, 0)
                            if n is not None:
                                pe.wait_ge(sem("normed"), 4 * PAIRS * b + 4 * p + (0 if s < 11 else 2))
                                if s >= 8 and p < 2:
                                    pe.wait_ge(sem("q_lo"), 4 * PAIRS * b + 4 * (p + 3))
                                if s == 15:
                                    pe.wait_ge(sem("shift_copied"), PAIRS * b + p + 2)
                                pe_early_turn(pe, n)
                            n = router_pair(p, s, 1)
                            if n is not None:
                                pe_early_logits(pe, n)
                                made[0] = n + 1
                        if not last_batch and p == 0 and s < ROW_PAIRS:
                            if s:
                                pe.wait_ge(sem("columns_ready"), ROW_PAIRS * (b + 1) + s)
                            pe_turn_rows(pe, b + 1, s, ps_x[:, :])
                        if not last_batch and p in (0, 1) and s == L_STEP:
                            pe.wait_ge(sem("shift_copied"), PAIRS * b + p + 2)
                            pe_latents(pe, b + 1, p, ps_x[:, :])
                        if not last_batch and p in (1, 2) and s == 0:
                            pe_turn_latents(pe, b + 1, p - 1, ps_x[:, :])
                        if s == 9:
                            if queries_next(p):
                                pe.wait_ge(sem("q_lo"), 4 * PAIRS * b + 4 * (p + 3))
                            else:
                                pe.wait_ge(sem("normed"), 4 * PAIRS * b + 4 * p)
                            denominators(p, 0)
                values(PAIRS - 1, STEPS - 1)
                def project(t):
                    if t >= 2:
                        pe.wait_ge(sem("att_added"), QT * b + t - 1)
                    else:
                        pe.wait_ge(sem("max_taken"), MAXES * PAIRS * b + MAXES * (PAIRS + (not last_batch)))
                    for p in range(PAIRS):
                        last = nc.tensor.matmul(ps_m[t % 2][:, 0:D], att_o[:, p, t * P:(t + 1) * P], w_vo[:, p, :],
                                                start=(p == 0), stop=(p == PAIRS - 1))
                    last.then_inc(sem("projected"), 1)
                pe.wait_ge(sem("normed"), 4 * PAIRS * b + 4 * PAIRS - 2)
                for t in range(QT):
                    if t == 2:
                        if not last_batch:
                            pe.wait_ge(sem("shift_copied"), PAIRS * b + PAIRS + 1)
                        denominators(PAIRS - 1, 1)
                    if t in (4, 6):
                        pe.wait_ge(sem("normed"), 4 * PAIRS * b + 4 * PAIRS + (t - 6) // 2)
                    project(t)
                pe.wait_ge(sem("att_added"), QT * b + QT)

            with pe.Fori(0, BATCH - 1) as b:
                batch(b)
            batch(BATCH - 1)

        def act_attention(act):
            act_std(act, "att", 0, QT)
            for i in range(ROW_PAIRS):
                act_columns(act, 0, i, banks[i])
            for j in range(2):
                act_latents(act, 0, j, banks[4 + j])
            for n in range(4):
                act_queries(act, n // 2, n % 2, n, banks[n])
            act_shift(act, 0)
            act_std(act, "att", QT, NT, 1)
            def batch(b):
                last_batch = isinstance(b, int)

                def max_next(p):
                    return not (last_batch and p == PAIRS - 1)

                def queries_next(p):
                    return not (last_batch and p >= PAIRS - 2)

                def exps(p, s):
                    c, kt = s // KT, s % KT
                    n = p * STEPS + s
                    act.wait_ge(sem("scored"), STEP_B * b + n + 1)
                    k = 2 * p + c
                    if kt == 0:
                        if p:
                            act.wait_ge(sem("denoms"), 2 * PAIRS * b + 2 * (p - 1) + c + 1)
                    else:
                        g = k * (KT - 1) + kt - 1
                        used_sum = g - (1 if kt == 1 else 3 if kt == 2 else 2)
                        used_val = n - (2 if kt >= 3 else 2 if kt == 1 else 4)
                        if used_sum >= 0:
                            act.wait_ge(sem("summed"), SUM_B * b + used_sum + 1)
                            act.wait_ge(sem("valued"), STEP_B * b + used_val + 1)
                    dst = prob_sum[:, c, :, :] if kt == 0 else prob[:, kt % 2, :, :]
                    nc.scalar.activation(dst, ps_s[n % 2][:, :, :], ACT.Exp, scale=SCALE).then_inc(sem("exp_done"), 1)

                def copy_o(p, c):
                    act.wait_ge(sem("valued"), STEP_B * b + p * STEPS + (c + 1) * KT)
                    nc.scalar.activation(att_o[:, p, c * HALF:(c + 1) * HALF], ps_o[:, :], ACT.Copy) \
                        .then_inc(sem("o_copied"), 1)

                for p in range(PAIRS):
                    for s in range(STEPS):
                        if last_batch and p == PAIRS - 2 and s == 0:
                            act.wait_ge(sem("q_made"), 2 * PAIRS * BATCH)
                            act.dma_start(gu_sb, w_gu).then_inc(sem("experts_loaded_f2"), 16)
                            act.dma_start(dn_sb, w_dn).then_inc(sem("experts_loaded_f2"), 16)
                        if s == 14 and max_next(p):
                            act_shift(act, PAIRS * b + p + 1, b, p)
                        exps(p, s)
                        if last_batch and p == 0 and s == 0:
                            act_std(act, "f2", 0, 2 * EARLY)
                        if not last_batch and p == 0 and s < ROW_PAIRS:
                            act_columns(act, b + 1, s, ps_x[:, :])
                        if last_batch and router_pair(p, s, 0) is not None:
                            act_early_columns(act, router_pair(p, s, 0))
                        if not last_batch and p in (0, 1) and s == L_STEP:
                            act_latents(act, b + 1, p, ps_x[:, :])
                        if s == 0 and p:
                            copy_o(p - 1, 1)
                        if s == KT:
                            copy_o(p, 0)
                        if s in A_STEPS and queries_next(p):
                            c = A_STEPS.index(s)
                            act_queries(act, (p + 2) % PAIRS, c, 2 * PAIRS * b + 2 * (p + 2) + c, ps_x[:, :])
                copy_o(PAIRS - 1, 1)

            with act.Fori(0, BATCH - 1) as b:
                batch(b)
            batch(BATCH - 1)

        def dve_attention(dve):
            def gathered(t):
                dve_gathered(dve, "f1", t // RING, t % RING)
            for t in range(QT):
                gathered(t)
            dve_stats(dve, "att", 0, QT)
            for i in range(ROW_PAIRS):
                dve_norm_rows(dve, 0, i)
                gathered(QT + i)
            for j in range(2):
                dve_keys_lo(dve, 0, j, banks[4 + j])
                gathered(QT + ROW_PAIRS + j)
            for j in range(2):
                dve_latent_rows(dve, 0, j, banks[4 + j])
            def queries(n):
                for a in range(2):
                    dve_queries(dve, n // 2, n % 2, a, n, banks[n])
            queries(0)
            queries(1)
            for m in range(MAXES):
                dve_max(dve, m, m)
                if m in (3, 6):
                    queries(m // 3 + 1)
                for t in range(BACK + m * (NT - BACK) // MAXES, BACK + (m + 1) * (NT - BACK) // MAXES):
                    gathered(t)
            dve_shift(dve, MAXES, 0)
            dve_stats(dve, "att", QT, NT, 1)
            def batch(b):
                last_batch = isinstance(b, int)

                def max_next(p):
                    return not (last_batch and p == PAIRS - 1)

                def queries_next(p):
                    return not (last_batch and p >= PAIRS - 2)

                def norm(p, c, h):
                    n = 2 * PAIRS * b + 2 * p + c
                    inv = ps_x[:, h * HALF // 2:(h + 1) * HALF // 2]
                    if h == 0:
                        dve.wait_ge(sem("denoms"), n + 1)
                        dve.wait_ge(sem("o_copied"), n + 1)
                    nc.vector.reciprocal(inv, inv).then_inc(sem("inverted"), 1)
                    dve.wait_ge(sem("inverted"), 2 * n + h + 1)
                    o = att_o[:, p, c * HALF + h * HALF // 2:c * HALF + (h + 1) * HALF // 2]
                    nc.vector.tensor_tensor(o, o, inv, ALU.mult).then_inc(sem("normed"), 1)

                for p in range(PAIRS):
                    for s in range(STEPS):
                        todo = list(range(max_at(s), max_at(s + 1))) if max_next(p) else []

                        def pieces(n):
                            for m in todo[:n]:
                                dve_max(dve, m, MAXES * PAIRS * b + MAXES * (p + 1) + m)
                            del todo[:n]
                        rests = [A_STEPS.index(s - 1)] if s - 1 in A_STEPS and queries_next(p) else []

                        def rest(a):
                            for c in rests:
                                dve_queries(dve, (p + 2) % PAIRS, c, a, 2 * PAIRS * b + 2 * (p + 2) + c, ps_x[:, :])
                        if not last_batch and p == 0 and s < ROW_PAIRS:
                            dve_norm_rows(dve, b + 1, s)
                        if last_batch and router_pair(p, s, 0) is not None:
                            dve_early_rows(dve, router_pair(p, s, 0))
                        pieces(1)
                        if last_batch and p == 0 and s == 0:
                            dve_variance(dve, "f2", 0, 2 * EARLY)
                        if last_batch and p == 0 and s == 1:
                            dve_scale(dve, "f2", 0, 2 * EARLY, 0)
                        if last_batch and router_pair(p, s, 2) is not None:
                            dve_keep_logits(dve, router_pair(p, s, 2))
                        if not last_batch and p in (1, 2):
                            if s == 0:
                                dve_keys_lo(dve, b + 1, p - 1, ps_x[:, :])
                            if s == 1:
                                dve_latent_rows(dve, b + 1, p - 1, ps_x[:, :])
                        rest(0)
                        if p and s in (3, 4):
                            norm(p - 1, 1, s - 3)
                        if s in (10, 11):
                            norm(p, 0, s - 10)
                        pieces(1)
                        rest(1)
                        pieces(1)
                        if s == 13 and max_next(p):
                            dve_shift(dve, MAXES * PAIRS * b + MAXES * (p + 2), PAIRS * b + p + 1)

                def add_projected(t):
                    dve.wait_ge(sem("projected"), QT * b + t + 1)
                    x = x_res[:, ds((b * QT + t) * D, D)]
                    nc.vector.tensor_tensor(x, x, ps_m[t % 2][:, 0:D], ALU.add).then_inc(sem("att_added"), 1)
                    dve.wait_ge(sem("att_added"), QT * b + t + 1)
                    tile_stats(b * QT + t, "f2")
                for t in range(QT):
                    if t in (2, 4):
                        norm(PAIRS - 1, 1, t // 2 - 1)
                    add_projected(t)

            with dve.Fori(0, BATCH - 1) as b:
                batch(b)
            batch(BATCH - 1)
            dve.wait_ge(sem("att_added"), NT)

        def pool_attention(pool):
            def batch(b):
                for p in range(PAIRS):
                    for c in range(2):
                        for kt in range(1, KT):
                            n = p * STEPS + c * KT + kt
                            k = 2 * p + c
                            pool.wait_ge(sem("exp_done"), STEP_B * b + n + 1)
                            if kt == 1:
                                pool.wait_ge(sem("valued"), STEP_B * b + n)
                            else:
                                pool.wait_ge(sem("summed"), SUM_B * b + k * (KT - 1) + kt - 1)
                            t = prob_sum[:, c, :, :].rearrange("p a n -> p (a n)")
                            nc.gpsimd.tensor_tensor(t, t, prob[:, kt % 2, :, :].rearrange("p a n -> p (a n)"), ALU.add) \
                                .then_inc(sem("summed"), 1)

            with pool.Fori(0, BATCH - 1) as b:
                batch(b)
            batch(BATCH - 1)

        def sp_attention(sp):
            def batch():
                for src, dst in ((keys_next, keys_now), (latent_next, latent_now)):
                    sp.dma_start(dst[:, :, :].bitcast(F32), src[:, :, :].bitcast(F32)).then_inc(sem("batch_ready"), 16)
            sp.wait_ge(sem("lat_rows"), 2)
            sp.wait_ge(sem("keys_fill"), 1)
            batch()
            sp.wait_ge(sem("q_hi"), 8)
            sp.wait_ge(sem("q_fill"), 1)
            sp_queries(sp, 0)
            sp_shift(sp, 0, 0)
            def pairs(b, last_batch):
                for p in range(PAIRS - last_batch):
                    if p:
                        sp.wait_ge(sem("scored"), STEP_B * b + STEPS * p)
                    sp_queries(sp, (p + 1) % PAIRS)
                    sp_shift(sp, (p + 1) % PAIRS, PAIRS * b + p + 1)
            with sp.Fori(0, BATCH - 1) as b:
                pairs(b, False)
                sp.wait_ge(sem("valued"), STEP_B * b + STEP_B)
                batch()
            pairs(BATCH - 1, True)
            sp.wait_ge(sem("batch_ready"), 32 * BATCH)
            for k in range(2):
                n = BATCH * PAIRS // 2
                sp.wait_ge(sem(f"q_copied{k}"), 16 * n)
                sp.wait_ge(sem(f"shift_placed{k}"), 32 * n)


        @block.sync
        def _(sp):
            for g in range(LOADS):
                n = NT // LOADS
                sp.dma_start(x_res[:, g * n * D:(g + 1) * n * D].rearrange("p (t d) -> p t d", d=D),
                             x_tiles[:, g * n:(g + 1) * n, :]).then_inc(sem(f"x_loaded{g}"), 16)
            sp.dma_start(gu_sb, w_gu).then_inc(sem("experts_loaded_f1"), 16)
            sp.dma_start(dn_sb, w_dn).then_inc(sem("experts_loaded_f1"), 16)
            sp_scaled_rows(sp, "f1")
            sp_attention(sp)
            sp_scaled_rows(sp, "f2")
            with sp.Fori(0, NT) as t:
                col = sp.snap(t * D)
                sp.wait_ge(sem("ffn_added_f2"), t + 1)
                sp.dma_start(out_tiles[:, ds(t, 1), :], x_res[:, ds(col, D)].unsqueeze(1)) \
                    .then_inc(sem("out_stored"), 16)
            sp.wait_ge(sem("out_stored"), 16 * NT)

        @block.gpsimd
        def _(pool):
            def mask(dst, compare, name, fill, base):
                pool.affine_select(out=base, in_=base, pattern=[[-1, P]], compare_op=compare, fill=fill,
                                   base=0, channel_multiplier=1).then_inc(sem(name), 1)
            pool.memset(ones[:, :], 1.0).then_inc(sem("filled"), 1)
            pool.memset(ident[:, :], 0.0).then_inc(sem("filled"), 1)
            pool.memset(before[:, :], 0.0).then_inc(sem("filled"), 1)
            pool.wait_ge(sem("filled"), 3)
            mask(ident, ALU.not_equal, "masks", 1.0, ident[:, :])
            mask(before, ALU.is_ge, "masks", 1.0, before[:, :])
            pool.iota(small[:, 7, :], [[-1, EXPERTS]], base=EXPERTS, channel_multiplier=0,
                      allow_small_or_imprecise_dtypes=True).then_inc(sem("masks"), 1)
            for table, pattern, slope in ((count_p, [[1, P]], 0), (row0, [[P, SLOT_TILES]], 0), (my_p, [[0, 1]], 1)):
                pool.iota(table[:, :], pattern, base=0, channel_multiplier=slope,
                          allow_small_or_imprecise_dtypes=True).then_inc(sem("tables"), 1)
            pool_split_weights(pool, "f1")
            pool_sorted_rows(pool, "f1")
            pool_gather(pool, "f1")
            pool_attention(pool)
            pool.wait_ge(sem("valued"), STEP_B * BATCH)
            pool_split_weights(pool, "f2")
            pool_sorted_rows(pool, "f2")
            pool_gather(pool, "f2")

        @block.vector
        def _(dve):
            for tag in ("f1", "f2"):
                dve_rows(dve, tag)
                if tag == "f1":
                    dve.wait_ge(sem("masks"), 3)
                    dve.wait_ge(sem("tables"), 3)
                ends = dve_route(dve, tag)
                dve_tile_experts(dve, tag, ends)
                if tag == "f1":
                    nc.vector.memset(keys_next[HD:P, 1, :].bitcast(F32), 0.0).then_inc(sem("keys_zero"), 1)
                    dve.wait_ge(sem("keys_zero"), 1)
                    nc.vector.memset(keys_next[HD:HD + 2, 1, :].bitcast(F32), 1.0).then_inc(sem("keys_fill"), 1)
                dve_experts(dve, tag)
                if tag == "f1":
                    dve_attention(dve)
                else:
                    dve_gather(dve)

        @block.scalar
        def _(act):
            act.dma_start(gate_w[:, :, :], gate_t).then_inc(sem("consts_loaded"), 16)
            for half in range(2):
                act.dma_start(kvd[:, :, half * HD:(half + 1) * HD], w_kvd).then_inc(sem("consts_loaded"), 16)
            for dst, src in ((q_raw, w_q), (k_raw, w_k), (v_raw, w_v), (o_raw, w_o_t)):
                act.dma_start(dst, src).then_inc(sem("raw_loaded"), 16)
            act_std(act, "f1", 0, NT // LOADS)
            act_transposed(act, "f1")
            act_exp_top(act, "f1")
            act_scaled_rows(act, "f1")
            act_experts(act, "f1")
            for p in range(PAIRS):
                for a in range(2):
                    act.wait_ge(sem("folded"), 4 * p + 2 * a + 1)
                    nc.scalar.activation(w_qk[:, :, p, a * HD:(a + 1) * HD],
                                         banks[5 + a].rearrange("p (c n) -> p c n", c=DC)[:, :, 0:HD], ACT.Copy) \
                        .then_inc(sem("fold_copied"), 1)
                    act.wait_ge(sem("folded"), 4 * p + 2 * a + 2)
                    nc.scalar.activation(w_vo[a * HD:(a + 1) * HD, p, :], banks[FOLD_O[a]][a * HD:(a + 1) * HD, 0:D],
                                         ACT.Copy) \
                        .then_inc(sem("fold_copied"), 1)
            act_attention(act)
            act_std(act, "f2", 2 * EARLY, NT, 1)
            act_transposed(act, "f2")
            act_exp_top(act, "f2")
            act_scaled_rows(act, "f2")
            act_experts(act, "f2")

        @block.tensor
        def _(pe):
            pe.wait_ge(sem("consts_loaded"), 48)
            pe.wait_ge(sem("masks"), 3)
            pe_transposed(pe, "f1")
            pe_ranks(pe, "f1")
            pe_tokens(pe, "f1")
            pe_experts(pe, "f1")
            pe.wait_ge(sem("y_ready_f1"), SLOT_TILES)
            pe.wait_ge(sem("raw_loaded"), 64)
            for p in range(PAIRS):
                for a in range(2):
                    h = slice(a * HD, (a + 1) * HD)
                    if p:
                        pe.wait_ge(sem("fold_copied"), 4 * (p - 1) + 2 * a + 2)
                    for c in range(DC):
                        last = nc.tensor.matmul(banks[5 + a][:, 256 * c:256 * c + HD], q_raw[h, p, c * P:(c + 1) * P],
                                                k_raw[h, p, :], start=True, stop=True)
                    last.then_inc(sem("folded"), 1)
                    nc.tensor.matmul(banks[FOLD_O[a]][h, 0:D], v_raw[h, p, :], o_raw[h, p, :],
                                     start=True, stop=True).then_inc(sem("folded"), 1)
            pe.wait_ge(sem("fold_copied"), 4 * PAIRS)
            pe_attention(pe)
            pe_transposed(pe, "f2")
            pe_ranks(pe, "f2")
            pe_tokens(pe, "f2")
            pe_experts(pe, "f2")


_OUT = ((BATCH, SEQ, D), "float32")


def kernel(L0_attn_x, L0_attn_Wq, L0_attn_Wkv_down, L0_attn_Wk_up, L0_attn_Wv_up, L0_attn_Wo,
           L0_ffn_gate_w, L0_ffn_w_gate, L0_ffn_w_up, L0_ffn_w_down):
    import numpy as np
    import concourse.bacc as bacc
    from concourse.bass_utils import run_bass_kernel_spmd

    def rows(w):
        w = np.asarray(w)
        return w.reshape(-1, P, w.shape[-1]).transpose(1, 0, 2)

    gu = np.concatenate([np.asarray(L0_ffn_w_gate), np.asarray(L0_ffn_w_up)], axis=1)
    arrays = {
        "x_in": np.asarray(L0_attn_x),
        "gate_t": rows(np.asarray(L0_ffn_gate_w).T),
        "w_gu": gu.reshape(EXPERTS, 2 * INNER, DC, P).transpose(3, 0, 2, 1),
        "w_dn": np.asarray(L0_ffn_w_down).transpose(2, 0, 1),
        "w_q": rows(L0_attn_Wq),
        "w_k": rows(L0_attn_Wk_up),
        "w_v": rows(L0_attn_Wv_up),
        "w_o_t": rows(np.asarray(L0_attn_Wo).T),
        "w_kvd": rows(np.asarray(L0_attn_Wkv_down).T),
    }
    arrays = {name: np.ascontiguousarray(a) for name, a in arrays.items()}
    nc = bacc.Bacc("TRN2", target_bir_lowering=False, num_devices=1)
    args = [nc.dram_tensor(name, a.shape, F32, kind="ExternalInput").ap() for name, a in arrays.items()]
    out = nc.dram_tensor("out", _OUT[0], F32, kind="ExternalOutput").ap()
    build(nc, *args, out)
    r = run_bass_kernel_spmd(nc, [arrays], core_ids=[0])
    return r.results[0]["out"]
```
